# Optimizing a Trainium2 kernel written in Bass

```python
import numpy as np
import jax
import jax.numpy as jnp

def _softmax(x, axis=-1):
    return jax.nn.softmax(x, axis=axis)

def _gelu(x):
    return jax.nn.gelu(x, approximate=True)

def _silu(x):
    return jax.nn.silu(x)

def _sigmoid(x):
    return jax.nn.sigmoid(x)

def _layernorm(x, axis=-1, eps=1e-05):
    m = jnp.mean(x, axis=axis, keepdims=True)
    v = jnp.var(x, axis=axis, keepdims=True)
    return (x - m) / jnp.sqrt(v + eps)

def _scatter_add(tgt, idx, src, axis=0):
    return tgt.at[idx].add(src)

def _segment_sum(src, seg, n):
    return jax.ops.segment_sum(src, seg, n)
kernel_name = 'mk_sandwich_d1_jaxref_r8_be3f50'

def setup_inputs(seed: int=0):
    np.random.seed(seed)
    _w = jnp.asarray

    def _L0_attn_setup():
        import jax, jax.numpy as jnp
        import numpy as np
        B, T, E = (2, 256, 128)
        H, D = (8, 64)
        ROPE_BASE = 10000.0

        def apply_rope(x):
            t = x.shape[2]
            d = x.shape[3]
            inv_freq = 1.0 / ROPE_BASE ** (jnp.arange(0, d, 2, dtype=jnp.float32) / d)
            ang = jnp.arange(t, dtype=jnp.float32)[:, None] * inv_freq[None, :]
            cos = jnp.cos(ang)[None, None].astype(x.dtype)
            sin = jnp.sin(ang)[None, None].astype(x.dtype)
            x1, x2 = jnp.split(x, 2, axis=-1)
            return jnp.concatenate([x1 * cos - x2 * sin, x1 * sin + x2 * cos], axis=-1)
        key = jax.random.key(seed)
        ks = jax.random.split(key, 5)
        s_in = 1.0 / np.sqrt(E)
        s_out = 1.0 / np.sqrt(H * D)
        return {'x': jax.random.normal(ks[0], (B, T, E), dtype=jnp.float32), 'Wq': jax.random.normal(ks[1], (H * D, E), dtype=jnp.float32) * s_in, 'Wk': jax.random.normal(ks[2], (H * D, E), dtype=jnp.float32) * s_in, 'Wv': jax.random.normal(ks[3], (H * D, E), dtype=jnp.float32) * s_in, 'Wo': jax.random.normal(ks[4], (E, H * D), dtype=jnp.float32) * s_out}
    _L0_attn_in = _L0_attn_setup()

    def _L0_ffn_setup():
        import jax, jax.numpy as jnp
        import numpy as np
        B, T, D, E, H = (4, 256, 128, 4, 8)
        EPS = 1e-05

        def _uniform(k, shape, bound):
            return jax.random.uniform(k, shape, jnp.float32, -bound, bound)

        def _layernorm(x, w, b):
            mu = jnp.mean(x, axis=-1, keepdims=True)
            var = jnp.mean(jnp.square(x - mu), axis=-1, keepdims=True)
            return (x - mu) * jax.lax.rsqrt(var + EPS) * w + b
        key = jax.random.key(seed)
        ks = jax.random.split(key, 12)
        wb = np.sqrt(6.0 / D) / np.sqrt(6.0)
        wb = 1.0 / np.sqrt(D)
        return {'x': jax.random.normal(ks[0], (B, T, D), jnp.float32), 'router_prob': jax.random.uniform(ks[1], (B, T, E), jnp.float32), 'norm_w': jnp.ones((D,), jnp.float32), 'norm_b': jnp.zeros((D,), jnp.float32), 'q_w': _uniform(ks[2], (D, D), wb), 'q_b': _uniform(ks[3], (D,), wb), 'k_w': _uniform(ks[4], (D, D), wb), 'k_b': _uniform(ks[5], (D,), wb), 'v_w': _uniform(ks[6], (D, D), wb), 'v_b': _uniform(ks[7], (D,), wb), 'o_w': _uniform(ks[8], (D, D), wb), 'o_b': _uniform(ks[9], (D,), wb)}
    _L0_ffn_in = _L0_ffn_setup()
    _d = {'L0_attn_x': _L0_attn_in['x'], 'L0_attn_Wq': _L0_attn_in['Wq'], 'L0_attn_Wk': _L0_attn_in['Wk'], 'L0_attn_Wv': _L0_attn_in['Wv'], 'L0_attn_Wo': _L0_attn_in['Wo'], 'L0_ffn_router_prob': _L0_ffn_in['router_prob'], 'L0_ffn_norm_w': _L0_ffn_in['norm_w'], 'L0_ffn_norm_b': _L0_ffn_in['norm_b'], 'L0_ffn_q_w': _L0_ffn_in['q_w'], 'L0_ffn_q_b': _L0_ffn_in['q_b'], 'L0_ffn_k_w': _L0_ffn_in['k_w'], 'L0_ffn_k_b': _L0_ffn_in['k_b'], 'L0_ffn_v_w': _L0_ffn_in['v_w'], 'L0_ffn_v_b': _L0_ffn_in['v_b'], 'L0_ffn_o_w': _L0_ffn_in['o_w'], 'L0_ffn_o_b': _L0_ffn_in['o_b']}
    _x0 = _d['L0_attn_x']
    _d['L0_attn_x'] = jax.random.normal(jax.random.fold_in(jax.random.key(seed), 1), (8, 1024, 128), dtype=_x0.dtype)
    del _x0
    return _d

def reference(L0_attn_x, L0_attn_Wq, L0_attn_Wk, L0_attn_Wv, L0_attn_Wo, L0_ffn_router_prob, L0_ffn_norm_w, L0_ffn_norm_b, L0_ffn_q_w, L0_ffn_q_b, L0_ffn_k_w, L0_ffn_k_b, L0_ffn_v_w, L0_ffn_v_b, L0_ffn_o_w, L0_ffn_o_b):

    def _L0_attn_ref(x, Wq, Wk, Wv, Wo):
        import jax, jax.numpy as jnp
        import numpy as np
        B, T, E = (2, 256, 128)
        H, D = (8, 64)
        ROPE_BASE = 10000.0

        def apply_rope(x):
            t = x.shape[2]
            d = x.shape[3]
            inv_freq = 1.0 / ROPE_BASE ** (jnp.arange(0, d, 2, dtype=jnp.float32) / d)
            ang = jnp.arange(t, dtype=jnp.float32)[:, None] * inv_freq[None, :]
            cos = jnp.cos(ang)[None, None].astype(x.dtype)
            sin = jnp.sin(ang)[None, None].astype(x.dtype)
            x1, x2 = jnp.split(x, 2, axis=-1)
            return jnp.concatenate([x1 * cos - x2 * sin, x1 * sin + x2 * cos], axis=-1)
        b, t, e = x.shape
        q = (x @ Wq.T).reshape(b, t, H, D).transpose(0, 2, 1, 3)
        k = (x @ Wk.T).reshape(b, t, H, D).transpose(0, 2, 1, 3)
        v = (x @ Wv.T).reshape(b, t, H, D).transpose(0, 2, 1, 3)
        q = apply_rope(q)
        k = apply_rope(k)
        scale = 1.0 / jnp.sqrt(jnp.asarray(D, dtype=x.dtype))
        scores = jnp.einsum('bhqd,bhkd->bhqk', q, k) * scale
        causal = jnp.tril(jnp.ones((t, t), dtype=bool))
        scores = jnp.where(causal[None, None], scores, jnp.asarray(-jnp.inf, dtype=scores.dtype))
        probs = jax.nn.softmax(scores, axis=-1)
        attn = jnp.einsum('bhqk,bhkd->bhqd', probs, v)
        out = attn.transpose(0, 2, 1, 3).reshape(b, t, H * D) @ Wo.T
        return out

    def _L0_ffn_ref(x, router_prob, norm_w, norm_b, q_w, q_b, k_w, k_b, v_w, v_b, o_w, o_b):
        import jax, jax.numpy as jnp
        import numpy as np
        B, T, D, E, H = (4, 256, 128, 4, 8)
        EPS = 1e-05

        def _uniform(k, shape, bound):
            return jax.random.uniform(k, shape, jnp.float32, -bound, bound)

        def _layernorm(x, w, b):
            mu = jnp.mean(x, axis=-1, keepdims=True)
            var = jnp.mean(jnp.square(x - mu), axis=-1, keepdims=True)
            return (x - mu) * jax.lax.rsqrt(var + EPS) * w + b
        e_cnt = router_prob.shape[2]
        b, t, d = x.shape
        n = t // e_cnt
        h = H
        scale = d ** (-0.5)
        qs, ks_, vs = ([], [], [])
        for e in range(e_cnt):
            xe = x[:, e * n:(e + 1) * n, :]
            xn = _layernorm(xe, norm_w, norm_b)
            m = d // 2 ** e
            xm = xn[..., :m]
            qs.append(jnp.einsum('bnm,dm->bnd', xm, q_w[:, :m]) + q_b)
            ks_.append(jnp.einsum('bnm,dm->bnd', xm, k_w[:, :m]) + k_b)
            vs.append(jnp.einsum('bnm,dm->bnd', xm, v_w[:, :m]) + v_b)
        q = jnp.concatenate(qs, axis=1)
        k = jnp.concatenate(ks_, axis=1)
        v = jnp.concatenate(vs, axis=1)
        dh = d // h
        q = q.reshape(b, t, h, dh).transpose(0, 2, 1, 3)
        k = k.reshape(b, t, h, dh).transpose(0, 2, 1, 3)
        v = v.reshape(b, t, h, dh).transpose(0, 2, 1, 3)
        attn = jnp.einsum('bhqd,bhkd->bhqk', q, k) * scale
        attn = jax.nn.softmax(attn, axis=-1)
        attn_out = jnp.einsum('bhqk,bhkd->bhqd', attn, v)
        attn_out = attn_out.transpose(0, 2, 1, 3).reshape(b, t, d)
        outs = []
        for e in range(e_cnt):
            sl = slice(e * n, (e + 1) * n)
            m = d // 2 ** e
            xm = attn_out[:, sl, :m]
            out = jnp.einsum('bnm,om->bno', xm, o_w[:m, :m]) + o_b[:m]
            pad = d - m
            if pad:
                out = jnp.pad(out, ((0, 0), (0, 0), (0, pad)))
            outs.append(out + x[:, sl, :])
        return jnp.concatenate(outs, axis=1)
    x = L0_attn_x
    x = x + _layernorm(_L0_attn_ref(_layernorm(x, axis=-1), L0_attn_Wq, L0_attn_Wk, L0_attn_Wv, L0_attn_Wo), axis=-1)
    x = x + _layernorm(_L0_ffn_ref(_layernorm(x, axis=-1), L0_ffn_router_prob, L0_ffn_norm_w, L0_ffn_norm_b, L0_ffn_q_w, L0_ffn_q_b, L0_ffn_k_w, L0_ffn_k_b, L0_ffn_v_w, L0_ffn_v_b, L0_ffn_o_w, L0_ffn_o_b), axis=-1)
    return x

_drawn_inputs = setup_inputs


def setup_inputs(seed=0):
    import zlib

    import numpy as np

    out = dict(_drawn_inputs(seed))
    spreads = {'L0_ffn_norm_w': (1.0, 0.6), 'L0_ffn_norm_b': (0.0, 0.8)}
    factors = {'L0_ffn_q_w': 8.0,
     'L0_ffn_q_b': 8.0,
     'L0_ffn_k_w': 8.0,
     'L0_ffn_k_b': 64.0,
     'L0_ffn_v_w': 4.037,
     'L0_ffn_v_b': 8.0,
     'L0_ffn_o_w': 3.787,
     'L0_ffn_o_b': 10.191}
    for name, (base, spread) in spreads.items():
        noise = np.random.default_rng([zlib.crc32(name.encode()), seed]).standard_normal(out[name].shape)
        drawn = base * np.exp(spread * noise) if base else spread * noise
        out[name] = jnp.asarray(drawn.astype(out[name].dtype))
    for name, factor in factors.items():
        out[name] = (out[name] * factor).astype(out[name].dtype)
    return out
```

```python
from contextlib import ExitStack

import concourse.bass as bass
from concourse import mybir

F32 = mybir.dt.float32
F32R = mybir.dt.float32r
BF16 = mybir.dt.bfloat16
ALU = mybir.AluOpType
ACT = mybir.ActivationFunctionType
AX_X = mybir.AxisListType.X

P = 128
B, T, E = 8, 1024, 128
H1, D1 = 8, 64
H2, D2 = 8, 16
EXPERTS = 4
NT = T // P
QT = 512
PAIRS, GROUPS = H1 // 2, H2 // 4
SCALE1, SCALE2 = D1 ** -0.5, E ** -0.5
EPS = 1e-5
NS, NP, NM = 3, 6, 3
UP, UG = 20, 64
SEL = 112
LOW_ONE = 2.0 ** -13
BIGNEG = -3.0e38


def width(t):
    return E >> (t * P // (T // EXPERTS))


def causal_units(qt):
    k = qt * 4
    return [[(kb, 0, 0)] for kb in range(k + 1)] + [[(k + 1, P, 0)], [(k + 2, 2 * P, 0), (k + 3, 3 * P, 2 * P)]]


UNITS1 = [(qt, blocks, h) for qt in range(2) for blocks in causal_units(qt) for h in range(2)]
assert len(UNITS1) == UP
QT0_UNITS = sum(qt == 0 for qt, _, _ in UNITS1)


def unit_width(blocks):
    kb, q0, c0 = blocks[-1]
    return c0 + QT - q0


def staged(jobs):
    out = [("stage", j) for j in jobs[:2]]
    for n, j in enumerate(jobs):
        out += [j] + [("stage", k) for k in jobs[n + 2:n + 3]]
    return out


def prep_pair(p):
    jobs = [("qk", p, t2) for t2 in range(4)]
    jobs += staged([("stk1", p, h, w, c) for h in range(2) for w in "qk" for c in range(2)])
    for h in range(2):
        jobs += [("max1", p, h, qb, c) for qb in range(NT) for c in range(2) if c == 0 or qb >= 4]
        jobs += [("dg1", p, h, 0)]
    return jobs


def prep_group(g):
    jobs = staged([("stk2", g, h, w, c) for h in range(4) for w in "qk" for c in range(2)])
    for h in range(4):
        jobs += [("max2", g, h, qb, c) for qb in range(NT) for c in range(2)]
        jobs += [("dg2", g, h), ("inj2", g, h, 0), ("inj2", g, h, 1)]
    return jobs


TAKE_IN = [("lnA",)] + [("y0T", c) for c in range(2)] + [("V", t) for t in range(NT)]
MIDDLE = ([("oproj", c) for c in range(2)] + [("xnT", c) for c in range(2)]
          + [("proj2", t) for t in range(NT)])
FINISH = ([("o2T", c, g) for c in range(2) for g in range(2)] + [("aoT", c) for c in range(2)]
          + [("fproj", c) for c in range(2)])


def spread(jobs, first, slots):
    out = {}
    for n, j in enumerate(jobs):
        out.setdefault(first + n * slots // len(jobs), []).append(j)
    return out


def causal_phase(routed_follows):
    side = {}
    for p in range(PAIRS):
        if p + 1 < PAIRS:
            jobs = prep_pair(p + 1)
        else:
            jobs = prep_group(0) if routed_follows else []
        if p == 0 and routed_follows:
            jobs = MIDDLE + jobs
        for u, js in spread(jobs, UP * p, UP).items():
            side.setdefault(u, []).extend(js)
        for h in range(2):
            side.setdefault(UP * p + 1, []).insert(0, ("dg1", p, 1 - h, 1))
        side.setdefault(UP * p + QT0_UNITS + 3, []).append(("sum1", p, 0))
        if p:
            side.setdefault(UP * p + 3, []).append(("sum1", p - 1, 1))
    items = []
    for u in range(UP * PAIRS):
        items.append(("unit1", u))
        if u % 2 and u >= 3:
            items.append(("pv1", u - 3))
        items += side.get(u, [])
    return items + [("pv1", UP * PAIRS - 2), ("sum1", PAIRS - 1, 1)]


def routed_phase(causal_follows):
    side = dict(spread((TAKE_IN if causal_follows else []) + prep_group(1), 0, UG))
    if causal_follows:
        side.update(spread(prep_pair(0), UG, UG))
    side.setdefault(UG - 2, []).append(("oev", 0, 0))
    side.setdefault(UG + 2, []).append(("oev", 0, 1))
    side.setdefault(2 * UG - 2, []).append(("oev", 1, 0))
    items = []
    for u in range(UG * GROUPS):
        items.append(("unit2", u))
        if u % 4 == 1 and u >= 5:
            items.append(("pv2", u - 5))
        items += side.get(u, [])
    return items + [("pv2", UG * GROUPS - 4), ("oev", 1, 1)] + FINISH


PHASES = {
    "first": [("x1_free",), ("loadA",)] + TAKE_IN + prep_pair(0),
    "causal0": [("loadA",)] + causal_phase(False),
    "second": TAKE_IN + prep_pair(0),
    "causal": [("loadB",), ("loadA",)] + causal_phase(True),
    "routed": routed_phase(True) + [("store",)],
    "middle": [("loadB",)] + MIDDLE + prep_group(0),
    "routed_last": routed_phase(False) + [("store",)],
}

LINKS = {"sum1": 1, "lnA": 4, "dg1": 2, "dg2": 2, "oproj": 15, "o2T": 1, "fproj": 12}
NORMS = {"lnA": (4,), "oproj": (4, 10, 15), "fproj": (4, 11)}
ACT_FREES = ("y0T", "V", "xnT", "aoT")
PE_JOBS = ("sum1", "qk", "stk1", "max1", "stk2", "max2", "inj2", "oproj", "proj2", "o2T", "fproj") + ACT_FREES


def increments(item):
    k = item[0]
    if k == "unit1":
        qt, blocks, _ = UNITS1[item[1] % UP]
        adds = {0: 0, 1: 2 - qt}.get(blocks[0][0], len(blocks))
        return {"s_ready": 1, "exp_done": 1, **({"sum_done": adds} if adds else {})}
    if k == "unit2":
        return {"s_ready": 1, "exp_done": 1}
    if k in ("pv1", "pv2"):
        return {"pv_done": 2 if k == "pv1" else 4}
    if k in ("loadA", "loadB"):
        return {"xa_loaded" if k == "loadA" else "xb_loaded": 16}
    if k == "x1_free":
        return {"out_stored": 16}
    if k == "store":
        return {"out_stored": 32}
    if k == "oev":
        return {"evac_done": 1}
    if k == "stage":
        return {"stage_done": 1}
    out = {}
    if k in PE_JOBS:
        out["m_ready"] = 1
    if k in ACT_FREES or k in ("stk1", "stk2"):
        out["evac_done"] = 1
    if k not in ACT_FREES:
        out["vec_done"] = 1
    if k == "qk":
        out["rope_done"] = 1
    if k in NORMS:
        out["pow_done"] = len(NORMS[k])
    links = LINKS.get(k, 0) if k != "dg1" or item[3] == 0 else 0
    if links:
        out["link"] = links
    return out


SEMS = ("s_ready", "exp_done", "sum_done", "pv_done", "m_ready", "evac_done", "vec_done", "rope_done",
        "link", "xa_loaded", "xb_loaded", "out_stored", "stage_done", "pow_done")
TOTAL = {n: {s: sum(increments(i).get(s, 0) for i in items) for s in SEMS} for n, items in PHASES.items()}
AFTER = {}
for _n, _items in PHASES.items():
    _c = dict.fromkeys(SEMS, 0)
    for _i in _items:
        for _s, _k in increments(_i).items():
            _c[_s] += _k
            AFTER[_n, _s, _i] = _c[_s]


class Count:

    def __init__(self, phase, before, loop=None):
        self.phase, self.before, self.loop = phase, before, loop

    def plus(self, sem, k):
        v = sum(TOTAL[n][sem] for n in self.before) + k
        if self.loop is not None:
            v = self.loop * (TOTAL["causal"][sem] + TOTAL["routed"][sem]) + v
        return v

    def start(self, sem):
        return self.plus(sem, 0)

    def after(self, sem, item):
        return self.plus(sem, AFTER.get((self.phase, sem, item), 0))

    def known(self, sem, item):
        return (self.phase, sem, item) in AFTER


MISC = {n: [i for i in items if i[0] in PE_JOBS] for n, items in PHASES.items()}
MISC_AT = {n: {i: k for k, i in enumerate(items)} for n, items in MISC.items()}
STACKS = {n: [i for i in items if i[0] in ("stk1", "stk2")] for n, items in PHASES.items()}
ROPES = {n: [i for i in items if i[0] == "qk"] for n, items in PHASES.items()}


def causal_routed_kernel(nc, x, wqk, wv, wo, w2, ow, bias2, o_b, norm_w, norm_b, rope_c, rope_s,
                         ident_in, mask_in, split_in, out):
    with ExitStack() as ctx:
        def sb(name, shape, dt=F32):
            return ctx.enter_context(nc.sbuf_tensor(name, shape, dt))

        def bank(name):
            return ctx.enter_context(nc.psum_tensor(name, [P, QT], F32))

        wqk_sb = sb("wqk_sb", [P, PAIRS, 4 * D1])
        wv_sb = sb("wv_sb", [P, H1 * D1])
        wo_sb = sb("wo_sb", [P, PAIRS, E])
        w2_sb = sb("w2_sb", [P, 3 * E])
        ow_sb = sb("ow_sb", [P, E])
        bias2_bc = sb("bias2_bc", [P, 3 * E])
        ob_bc = sb("ob_bc", [P, E])
        norm_wb = sb("norm_wb", [P, 2])
        cos_sb = sb("cos_sb", [P, NT, D1 // 2])
        sin_sb = sb("sin_sb", [P, NT, D1])
        ident = sb("ident", [P, P])
        identb = sb("identb", [P, P], BF16)
        maskt = sb("maskt", [P, P], BF16)
        split = sb("split", [P, 2])
        ones_r = sb("ones_r", [P, P], F32R)
        ones = ones_r[:, 0:D1].bitcast(F32)
        sel_r = sb("sel_r", [P, P], F32R)
        xa = sb("xa", [P, NT, E])
        xb = sb("xb", [P, NT, E])
        o2 = [xa, xb]
        x1 = sb("x1", [P, NT, E])
        y1 = sb("y1", [P, 4, E])
        xn = sb("xn", [P, NT, E])
        y0t = sb("y0t", [P, T])
        xnt = sb("xnt", [P, T])
        v1 = sb("v1", [P, NT, H1 * D1])
        rq = sb("rq", [P, NT, 4, D1])
        rtmp = sb("rtmp", [P, 2, 4, D1])
        stage = sb("stage", [P, 2, 4, P])
        stk = sb("stk", [P, 2, 8, T], F32R)
        qkv2 = sb("qkv2", [P, NT, 3, H2, 2 * D2])
        probs = sb("probs", [P, NP, QT])
        ot = sb("ot", [P, PAIRS, T])
        dg = sb("dg", [P, 4, QT], F32R)
        acc = sb("acc", [P, 2, 2, QT])
        mx = sb("mx", [P, 2, NT, 2])
        mx2 = sb("mx2", [P, NT, 2])
        m8 = sb("m8", [P, 2, NT])
        m8n = sb("m8n", [P, 2, NT])
        st = sb("st", [P, NT, 6])
        sums = sb("sums", [P, NT, 2])
        diff = sb("diff", [P, NT])
        diff2 = sb("diff2", [P, NT])
        mean = sb("mean", [P, NT])
        vpart = sb("vpart", [P, NT])
        zero = sb("zero", [P, 1])
        var = sb("var", [P, NT])
        rstd = sb("rstd", [P, NT])
        neghalf = sb("neghalf", [P, NT])
        rz = sb("rz", [P, 4, 4])

        S = [bank(f"score{n}") for n in range(NS)]
        M = [bank(f"side{n}") for n in range(NM)]
        O = [bank(f"attn{n}") for n in range(2)]

        sems = {n: ctx.enter_context(nc.semaphore(n)) for n in SEMS}
        s_ready, exp_done, sum_done, pv_done = (sems[n] for n in SEMS[:4])
        m_ready, evac_done, vec_done, rope_done = (sems[n] for n in SEMS[4:8])
        link, xa_loaded, xb_loaded, out_stored, stage_done, pow_done = (sems[n] for n in SEMS[8:])
        w_loaded = ctx.enter_context(nc.semaphore("w_loaded"))
        const_done = ctx.enter_context(nc.semaphore("const_done"))
        vec_consts = ctx.enter_context(nc.semaphore("vec_consts"))

        def pair_ops(p, h):
            s = stk[:, p % 2]
            return s[:, 3 * h], s[:, 3 * h + 1], s[:, 3 * h + 2]

        def group_ops(g, h):
            s = stk[:, g % 2]
            return s[:, h], s[:, 4 + h]

        def misc(c, item):
            return M[MISC_AT[c.phase][item] % NM]

        WEIGHTS = 13

        def run(eng, phase):
            done = []
            for name, b1, b2 in (("first", 0, None), ("causal0", 0, None), ("second", 1, None)):
                phase(Count(name, list(done)), b1, b2)
                done.append(name)
            with eng.Fori(1, B) as i:
                minus = [n for n in done]
                phase(Count("causal", minus, i - 1), i, i - 1)
                phase(Count("routed", minus + ["causal"], i - 1), i, i - 1)
            done += ["causal", "routed"] * (B - 1)
            for name in ("middle", "routed_last"):
                phase(Count(name, list(done)), None, B - 1)
                done.append(name)
            return done

        block = ctx.enter_context(nc.Block())

        @block.sync
        def _(sp):
            sp.dma_start(ident[:], ident_in).then_inc(out_stored, 16)
            for dst, src in ((wv_sb, wv), (w2_sb, w2), (ow_sb, ow), (split, split_in)):
                sp.dma_start(dst[:], src).then_inc(w_loaded, 16)
            sp.dma_start(stage[:, 0, 0, :], mask_in).then_inc(w_loaded, 16)
            sp.dma_start(wqk_sb[:], wqk.rearrange("e (p n) -> e p n", p=PAIRS)).then_inc(w_loaded, 16)
            sp.dma_start(wo_sb[:], wo.rearrange("(p r) n -> r p n", r=P)).then_inc(w_loaded, 16)
            sp.dma_start(cos_sb[:], rope_c.rearrange("(t p) d -> p t d", p=P)).then_inc(w_loaded, 16)
            sp.dma_start(sin_sb[:], rope_s.rearrange("(t p) d -> p t d", p=P)).then_inc(w_loaded, 16)
            for dst, src in ((bias2_bc, bias2), (ob_bc, o_b)):
                sp.dma_start(dst[:], src.partition_broadcast(P)).then_inc(w_loaded, 16)
            for n, src in enumerate((norm_w, norm_b)):
                sp.dma_start(norm_wb[:, n:n + 1], src.unsqueeze(1)).then_inc(w_loaded, 16)

            xv = x.rearrange("(b t p) e -> b p t e", b=B, p=P)
            ov = out.rearrange("(b t p) e -> b p t e", b=B, p=P)

            def phase(c, b1, b2):
                for item in PHASES[c.phase]:
                    if item[0] == "loadA":
                        sp.wait_ge(m_ready, c.start("m_ready"))
                        b = 0 if c.phase == "first" else (b1 + 1) % B
                        sp.dma_start(xa[:], xv[b]).then_inc(xa_loaded, 16)
                    if item[0] == "loadB":
                        sp.wait_ge(m_ready, c.start("m_ready"))
                        sp.dma_start(xb[:], xv[b2]).then_inc(xb_loaded, 16)
                    if item[0] == "store":
                        for half in range(2):
                            sp.wait_ge(vec_done, c.after("vec_done", ("fproj", half)))
                            sp.dma_start(ov[b2][:, 4 * half:4 * half + 4], x1[:, 4 * half:4 * half + 4, :])\
                                .then_inc(out_stored, 16)

            done = run(sp, phase)
            sp.wait_ge(out_stored, sum(TOTAL[n]["out_stored"] for n in done))

        @block.tensor
        def _(pe):
            mm = nc.tensor.matmul

            def transpose4(dst, src_of):
                for t in range(4):
                    last = nc.tensor.transpose(dst[:, t * P:(t + 1) * P], src_of(t), ident[:])
                return last

            def unit1(c, item):
                u = item[1]
                p, (qt, blocks, h) = u // UP, UNITS1[u % UP]
                q_op, k_hi, k_lo = pair_ops(p, h)
                if u >= NS:
                    pe.wait_ge(exp_done, c.after("exp_done", ("unit1", u - NS)))
                pe.wait_ge(vec_done, c.after("vec_done", ("dg1", p, h, qt)))
                s = S[u % NS]
                for kb, q0, c0 in blocks:
                    n = QT - q0
                    ks = slice(kb * P, (kb + 1) * P)
                    qs = slice(qt * QT + q0, (qt + 1) * QT)
                    diagonal = kb >= 4 * qt
                    mm(s[:, c0:c0 + n], k_hi[:, ks], q_op[:, qs], start=True, stop=False)
                    mm(s[:, c0:c0 + n], k_lo[:, ks], q_op[:, qs], start=False, stop=False)
                    last = mm(s[:, c0:c0 + n], ones_r[:], dg[:, 2 * h + qt, q0:], start=False, stop=True)
                    if diagonal:
                        last = mm(s[:, c0:c0 + P], identb[:], maskt[:], start=False, stop=True,
                                  skip_group_check=True)
                last.then_inc(s_ready, 1)

            def pv1(c, item):
                u0 = item[1]
                p, (qt, blocks, _) = u0 // UP, UNITS1[u0 % UP]
                pe.wait_ge(exp_done, c.after("exp_done", ("unit1", u0 + 1)))
                if blocks[0][0] == 0:
                    before = ("sum1", p - 1, qt)
                    if c.known("vec_done", before):
                        pe.wait_ge(vec_done, c.after("vec_done", before))
                    else:
                        pe.wait_ge(evac_done, c.start("evac_done"))
                o = O[qt]
                for n, (kb, q0, c0) in enumerate(blocks):
                    for h in range(2):
                        last = mm(o[D1 * h:D1 * h + D1, q0:], v1[:, kb, (2 * p + h) * D1:(2 * p + h + 1) * D1],
                                  probs[:, (u0 + h) % NP, c0:c0 + QT - q0], start=(kb == 0),
                                  stop=(kb == 4 * qt + 3), skip_group_check=True)
                last.then_inc(pv_done, 2)

            def unit2(c, item):
                u = item[1]
                g, kb, qt, h = u // UG, u % UG // 8, u % 8 // 4, u % 4
                if u >= NS:
                    pe.wait_ge(exp_done, c.after("exp_done", ("unit2", u - NS)))
                if kb == 0:
                    pe.wait_ge(vec_done, c.after("vec_done", ("inj2", g, h, 1)))
                q_op, k_op = group_ops(g, h)
                mm(S[u % NS][:, :], k_op[:, kb * P:(kb + 1) * P], q_op[:, qt * QT:(qt + 1) * QT],
                   start=True, stop=True).then_inc(s_ready, 1)

            def pv2(c, item):
                u0 = item[1]
                g, kb, qt = u0 // UG, u0 % UG // 8, u0 % 8 // 4
                pe.wait_ge(exp_done, c.after("exp_done", ("unit2", u0 + 3)))
                if kb == 0 and g:
                    pe.wait_ge(evac_done, c.after("evac_done", ("oev", g - 1, qt)))
                for h in range(4):
                    last = mm(O[qt][32 * h:32 * h + 32, :], qkv2[:, kb, 2, 4 * g + h, :],
                              probs[:, (u0 + h) % NP, :], start=(kb == 0), stop=(kb == NT - 1),
                              skip_group_check=True)
                last.then_inc(pv_done, 4)

            def job(c, item):
                k = item[0]
                n = MISC_AT[c.phase][item]
                m = M[n % NM]
                if n >= NM:
                    old = MISC[c.phase][n - NM]
                    if old[0] in ACT_FREES:
                        pe.wait_ge(evac_done, c.after("evac_done", old))
                    else:
                        pe.wait_ge(vec_done, c.after("vec_done", old))
                if k == "y0T":
                    pe.wait_ge(vec_done, c.after("vec_done", ("lnA",)))
                    last = transpose4(m, lambda t: xa[:, 4 * item[1] + t, :])
                if k == "V":
                    t = item[1]
                    pe.wait_ge(evac_done, c.after("evac_done", ("y0T", t // 4)))
                    last = mm(m[:, :], y0t[:, t * P:(t + 1) * P], wv_sb[:], start=True, stop=True)
                if k == "qk":
                    _, p, t2 = item
                    if c.known("evac_done", ("y0T", 1)):
                        pe.wait_ge(evac_done, c.after("evac_done", ("y0T", 1)))
                    for j in range(2):
                        t = 2 * t2 + j
                        last = mm(m[:, 256 * j:256 * j + 256], y0t[:, t * P:(t + 1) * P], wqk_sb[:, p, :],
                                  start=True, stop=True)
                if k == "stk1":
                    _, p, h, w, half = item
                    pe.wait_ge(stage_done, c.after("stage_done", ("stage", item)))
                    last = transpose4(m, lambda t: stage[:, STACKS[c.phase].index(item) % 2, t, :])
                if k == "max1":
                    _, p, h, qb, half = item
                    q_op, k_hi, _ = pair_ops(p, h)
                    pe.wait_ge(vec_done, c.after("vec_done", ("stk1", p, h, "k", 1)))
                    end = min((qb + 1) * P, (half + 1) * QT)
                    w = end - half * QT
                    diagonal = end == (qb + 1) * P
                    last = mm(m[:, 0:w], q_op[:, qb * P:(qb + 1) * P], k_hi[:, half * QT:end],
                              start=True, stop=True)
                    if diagonal:
                        last = mm(m[:, w - P:w], maskt[:], identb[:], start=False, stop=True,
                                  skip_group_check=True)
                if k == "sum1":
                    _, p, qt = item
                    u = UP * p + (QT0_UNITS if qt == 0 else UP) - 1
                    pe.wait_ge(sum_done, c.after("sum_done", ("unit1", u)))
                    for h in range(2):
                        last = mm(m[D1 * h:D1 * h + D1, :], ones, acc[:, qt, h, :], start=True, stop=True,
                                  skip_group_check=True)
                if k == "stk2":
                    _, g, h, w, half = item
                    pe.wait_ge(stage_done, c.after("stage_done", ("stage", item)))
                    last = transpose4(m, lambda t: stage[:, STACKS[c.phase].index(item) % 2, t, :])
                if k == "max2":
                    _, g, h, qb, half = item
                    q_op, k_op = group_ops(g, h)
                    pe.wait_ge(vec_done, c.after("vec_done", ("stk2", g, h, "k", 1)))
                    last = mm(m[:, :], q_op[:, qb * P:(qb + 1) * P], k_op[:, half * QT:(half + 1) * QT],
                              start=True, stop=True)
                if k == "inj2":
                    _, g, h, qt = item
                    pe.wait_ge(vec_done, c.after("vec_done", ("dg2", g, h)))
                    last = mm(m[:, :], sel_r[:], dg[:, 2 * qt, :], start=True, stop=True)
                if k == "oproj":
                    for t in range(4):
                        q0 = (4 * item[1] + t) * P
                        for p in range(PAIRS):
                            last = mm(m[:, t * P:(t + 1) * P], ot[:, p, q0:q0 + P], wo_sb[:, p, :],
                                      start=(p == 0), stop=(p == PAIRS - 1))
                if k == "xnT":
                    pe.wait_ge(vec_done, c.after("vec_done", ("oproj", item[1])))
                    last = transpose4(m, lambda t: xn[:, 4 * item[1] + t, :])
                if k == "proj2":
                    t = item[1]
                    w = width(t)
                    pe.wait_ge(evac_done, c.after("evac_done", ("xnT", t // 4)))
                    last = mm(m[:, 0:3 * E], xnt[0:w, t * P:(t + 1) * P], w2_sb[0:w, :], start=True, stop=True)
                if k == "o2T":
                    _, half, g = item
                    pe.wait_ge(evac_done, c.after("evac_done", ("oev", g, half)))
                    last = transpose4(m, lambda t: o2[g][:, 4 * half + t, :])
                if k == "aoT":
                    pe.wait_ge(vec_done, c.after("vec_done", ("o2T", item[1], 1)))
                    last = transpose4(m, lambda t: xn[:, 4 * item[1] + t, :])
                if k == "fproj":
                    pe.wait_ge(evac_done, c.after("evac_done", ("aoT", item[1])))
                    for j in range(4):
                        t = 4 * item[1] + j
                        w = width(t)
                        last = mm(m[:, j * P:j * P + w], xnt[0:w, t * P:(t + 1) * P], ow_sb[0:w, 0:w],
                                  start=True, stop=True)
                last.then_inc(m_ready, 1)

            def phase(c, b1, b2):
                pe.wait_ge(exp_done, c.start("exp_done"))
                pe.wait_ge(vec_done, c.start("vec_done"))
                pe.wait_ge(evac_done, c.start("evac_done"))
                for item in PHASES[c.phase]:
                    if item[0] == "unit1":
                        unit1(c, item)
                    elif item[0] == "unit2":
                        unit2(c, item)
                    elif item[0] == "pv1":
                        pv1(c, item)
                    elif item[0] == "pv2":
                        pv2(c, item)
                    elif item[0] in PE_JOBS:
                        job(c, item)

            pe.wait_ge(w_loaded, 16 * WEIGHTS)
            pe.wait_ge(out_stored, 16)
            pe.wait_ge(vec_consts, 3)
            pe.wait_ge(const_done, 8)
            run(pe, phase)

        @block.scalar
        def _(act):
            def unit(c, item):
                k, u = item
                w = QT if k == "unit2" else unit_width(UNITS1[u % UP][1])
                act.wait_ge(s_ready, c.after("s_ready", item))
                if u >= NP:
                    if k == "unit1":
                        act.wait_ge(pv_done, c.after("pv_done", ("pv1", (u - NP) // 2 * 2)))
                        first = UNITS1[(u - NP) % UP][1][0][0] == 0
                        act.wait_ge(sum_done, c.after("sum_done", ("unit1", u - NP + 2 * first)))
                    else:
                        act.wait_ge(pv_done, c.after("pv_done", ("pv2", (u - NP) // 4 * 4)))
                nc.scalar.activation(probs[:, u % NP, 0:w], S[u % NS][:, 0:w], ACT.Exp,
                                     scale=SCALE1 if k == "unit1" else SCALE2).then_inc(exp_done, 1)

            def copy_to_stage(c, item):
                stk_item = item[1]
                k, b, h, w, half = stk_item
                n = STACKS[c.phase].index(stk_item)
                if n >= 2:
                    act.wait_ge(m_ready, c.after("m_ready", STACKS[c.phase][n - 2]))
                else:
                    act.wait_ge(m_ready, c.start("m_ready"))
                ts = slice(4 * half, 4 * half + 4)
                if k == "stk1":
                    act.wait_ge(rope_done, c.after("rope_done", ("qk", b, 2 * half + 1)))
                    src, times, d = rq[:, ts, "qk".index(w) * 2 + h, :], 2, D1
                else:
                    act.wait_ge(vec_done, c.after("vec_done", ("proj2", 4 * half + 3)))
                    src, times, d = qkv2[:, ts, "qk".index(w), 4 * b + h, :], 4, 2 * D2
                nc.scalar.copy(stage[:, n % 2].rearrange("p t (r d) -> p t r d", r=times),
                               src.unsqueeze(2).to_broadcast([P, 4, times, d])).then_inc(stage_done, 1)

            def job(c, item):
                k = item[0]
                if k == "oev":
                    _, g, qt = item
                    act.wait_ge(pv_done, c.after("pv_done", ("pv2", UG * g + UG - 8 + 4 * qt)))
                    if g == 0 and c.known("m_ready", ("y0T", 1)):
                        act.wait_ge(m_ready, c.after("m_ready", ("y0T", 1)))
                    if g == 1:
                        act.wait_ge(vec_done, c.start("vec_done"))
                    nc.scalar.copy(o2[g][:, 4 * qt:4 * qt + 4, :], O[qt][:, :]).then_inc(evac_done, 1)
                    return
                m = misc(c, item)
                act.wait_ge(m_ready, c.after("m_ready", item))
                if k == "y0T":
                    dst = y0t[:, item[1] * QT:(item[1] + 1) * QT]
                if k == "V":
                    dst = v1[:, item[1], :]
                if k in ("xnT", "aoT"):
                    dst = xnt[:, item[1] * QT:(item[1] + 1) * QT]
                if k in ("stk1", "stk2"):
                    _, b, h, w, half = item
                    ops = pair_ops(b, h) if k == "stk1" else group_ops(b, h)
                    dst = ops["qk".index(w)][:, half * QT:(half + 1) * QT]
                if k == "xnT":
                    nc.scalar.activation(dst, m[:, :], ACT.Identity, scale=norm_wb[:, 0:1],
                                         bias=norm_wb[:, 1:2]).then_inc(evac_done, 1)
                else:
                    nc.scalar.copy(dst, m[:, :]).then_inc(evac_done, 1)

            def phase(c, b1, b2):
                act.wait_ge(vec_done, c.start("vec_done"))
                act.wait_ge(pv_done, c.start("pv_done"))
                act.wait_ge(sum_done, c.start("sum_done"))
                for item in PHASES[c.phase]:
                    if item[0] in ("unit1", "unit2"):
                        unit(c, item)
                    elif item[0] == "stage":
                        copy_to_stage(c, item)
                    elif "evac_done" in increments(item):
                        job(c, item)

            act.wait_ge(w_loaded, 16 * WEIGHTS)
            act.wait_ge(out_stored, 16)
            act.wait_ge(vec_consts, 3)
            act.wait_ge(const_done, 8)
            run(act, phase)

        @block.gpsimd
        def _(pool):
            def unit1(c, item):
                u = item[1]
                p, (qt, blocks, h) = u // UP, UNITS1[u % UP]
                if blocks[0][0] == 0:
                    return
                pool.wait_ge(exp_done, c.after("exp_done", item))
                if blocks[0][0] == 1 and c.known("m_ready", ("sum1", p - 1, qt)):
                    pool.wait_ge(m_ready, c.after("m_ready", ("sum1", p - 1, qt)))
                a = acc[:, qt, h, :]
                if blocks[0][0] == 1:
                    first, src = probs[:, (u - 2) % NP, :], probs[:, u % NP, :]
                    q0 = blocks[0][1]
                    if q0:
                        nc.gpsimd.tensor_tensor(a[:, 0:q0], first[:, 0:q0], zero[:].to_broadcast([P, q0]), ALU.add)\
                            .then_inc(sum_done, 1)
                    nc.gpsimd.tensor_tensor(a[:, q0:], first[:, q0:], src[:, 0:QT - q0], ALU.add).then_inc(sum_done, 1)
                    return
                for n, (kb, q0, c0) in enumerate(blocks):
                    if n:
                        pool.wait_ge(sum_done, c.plus("sum_done", AFTER[c.phase, "sum_done", item] - 1))
                    else:
                        pool.wait_ge(sum_done, c.after("sum_done", ("unit1", u - 2)))
                    nc.gpsimd.tensor_tensor(a[:, q0:], a[:, q0:], probs[:, u % NP, c0:c0 + QT - q0], ALU.add)\
                        .then_inc(sum_done, 1)

            def qk(c, item):
                _, p, t2 = item
                pool.wait_ge(vec_done, c.after("vec_done", item))
                r = rq[:, 2 * t2:2 * t2 + 2].rearrange("p t h d -> p (t h d)")
                s = rtmp[:].rearrange("p t h d -> p (t h d)")
                nc.gpsimd.tensor_tensor(r, r, s, ALU.add).then_inc(rope_done, 1)

            def powers(c, item):
                k = item[0]
                tiles = slice(0, NT) if k == "lnA" else slice(4 * item[1], 4 * item[1] + 4)
                for step in NORMS[k]:
                    at = AFTER[c.phase, "link", item] - LINKS[k] + step
                    pool.wait_ge(link, c.plus("link", at))
                    nc.gpsimd.tensor_tensor(rstd[:, tiles], var[:, tiles], neghalf[:, tiles], ALU.pow)\
                        .then_inc(pow_done, 1)

            def phase(c, b1, b2):
                pool.wait_ge(m_ready, c.start("m_ready"))
                for item in PHASES[c.phase]:
                    if item[0] == "unit1":
                        unit1(c, item)
                    elif item[0] == "qk":
                        qk(c, item)
                    elif item[0] in NORMS:
                        powers(c, item)

            nc.gpsimd.memset(ones_r[:].bitcast(F32), 1.0).then_inc(const_done, 1)
            nc.gpsimd.memset(sel_r[:].bitcast(F32), 0.0).then_inc(const_done, 1)
            nc.gpsimd.memset(qkv2[:], 0.0).then_inc(const_done, 1)
            nc.gpsimd.memset(neghalf[:], -0.5).then_inc(const_done, 1)
            nc.gpsimd.memset(zero[:], 0.0).then_inc(const_done, 1)
            pool.wait_ge(const_done, 5)
            nc.gpsimd.memset(sel_r[:, SEL:SEL + 1].bitcast(F32), 1.0).then_inc(const_done, 1)
            nc.gpsimd.memset(qkv2[:, :, 1, :, D2:D2 + 1], 1.0 + LOW_ONE).then_inc(const_done, 1)
            nc.gpsimd.memset(qkv2[:, :, 2, :, D2:D2 + 1], 1.0).then_inc(const_done, 1)
            run(pool, phase)

        @block.vector
        def _(dve):
            V = nc.vector

            class Chain:

                def __init__(self, c, item):
                    self.c, self.item, self.n, self.norms = c, item, 0, 0

                def wait(self):
                    self.n += 1
                    all_links = increments(self.item)["link"]
                    at = AFTER[self.c.phase, "link", self.item] - all_links + self.n
                    dve.wait_ge(link, self.c.plus("link", at))

                def wait_pow(self):
                    self.n += 1
                    self.norms += 1
                    k = self.item[0]
                    assert NORMS[k][self.norms - 1] == self.n
                    at = AFTER[self.c.phase, "pow_done", self.item] - len(NORMS[k]) + self.norms
                    dve.wait_ge(pow_done, self.c.plus("pow_done", at))

            def layer_norm(ch, src, dst, tiles):
                for t in tiles:
                    last = V.bn_stats(st[:, t, :], src(t))
                last.then_inc(link, 1)
                ch.wait()
                a, b = tiles[0], tiles[-1] + 1
                ts = slice(a, b)
                V.tensor_tensor(sums[:, ts, :], st[:, ts, 1:3], st[:, ts, 4:6], ALU.add)
                V.tensor_tensor(diff[:, ts], st[:, ts, 1], st[:, ts, 4], ALU.subtract).then_inc(link, 1)
                ch.wait()
                V.tensor_scalar(mean[:, ts], sums[:, ts, 0], 0.5, None, ALU.mult)
                V.tensor_scalar(vpart[:, ts], sums[:, ts, 1], 1.0 / E, EPS, ALU.mult, ALU.add)
                V.tensor_tensor(diff2[:, ts], diff[:, ts], diff[:, ts], ALU.mult).then_inc(link, 1)
                ch.wait()
                V.scalar_tensor_tensor(out=var[:, ts], in0=diff2[:, ts], scalar=0.25, in1=vpart[:, ts],
                                       op0=ALU.mult, op1=ALU.add).then_inc(link, 1)
                ch.wait_pow()
                for t in tiles:
                    last = V.tensor_scalar(dst(t), src(t), mean[:, t:t + 1], rstd[:, t:t + 1], ALU.subtract, ALU.mult)
                return last

            def job(c, item):
                k = item[0]
                ch = Chain(c, item)
                m = None
                if k in PE_JOBS:
                    m = misc(c, item)
                    dve.wait_ge(m_ready, c.after("m_ready", item))
                if k not in ("max1", "max2"):
                    dve.wait_ge(vec_done, c.plus("vec_done", AFTER[c.phase, "vec_done", item] - 1))
                if k == "lnA":
                    dve.wait_ge(xa_loaded, c.start("xa_loaded") if c.phase != "first" else 16)
                    last = layer_norm(ch, lambda t: xa[:, t, :], lambda t: xa[:, t, :], range(NT))
                if k == "qk":
                    _, p, t2 = item
                    n = ROPES[c.phase].index(item)
                    if n:
                        dve.wait_ge(rope_done, c.after("rope_done", ROPES[c.phase][n - 1]))
                    mv4 = m[:, :].rearrange("p (t h d) -> p t h d", t=2, h=4)
                    s = rtmp[:]
                    hd = D1 // 2
                    ts = slice(2 * t2, 2 * t2 + 2)
                    cosb = cos_sb[:, ts, :].unsqueeze(2).to_broadcast([P, 2, 8, hd])
                    V.tensor_tensor(rq[:, ts].rearrange("p t h (x d) -> p t (h x) d", x=2),
                                    m[:, :].rearrange("p (t h d) -> p t h d", t=2, h=8), cosb, ALU.mult)
                    for lo, hi in ((0, hd), (hd, 0)):
                        sinb = sin_sb[:, ts, lo:lo + hd].unsqueeze(2).to_broadcast([P, 2, 4, hd])
                        last = V.tensor_tensor(s[:, :, :, lo:lo + hd], mv4[:, :, :, hi:hi + hd], sinb, ALU.mult)
                if k == "stk1" and item[3] == "k":
                    _, p, h, _, half = item
                    dve.wait_ge(evac_done, c.after("evac_done", item))
                    _, hi, lo = pair_ops(p, h)
                    cs = slice(half * QT, (half + 1) * QT)
                    last = V.tensor_tensor(lo[:, cs], m[:, :], hi[:, cs].bitcast(F32), ALU.subtract)
                elif k in ("stk1", "stk2"):
                    _, b, h, w, half = item
                    dve.wait_ge(evac_done, c.after("evac_done", item))
                    if k == "stk1":
                        dst = pair_ops(b, h)[0]
                    else:
                        dst = group_ops(b, h)["qk".index(w)]
                    low = 1 if (k == "stk2" and w == "k") else 0
                    dst = dst[:, half * QT:(half + 1) * QT]
                    last = V.scalar_tensor_tensor(out=dst, in0=dst.bitcast(F32),
                                                  scalar=split[:, low:low + 1], in1=m[:, :],
                                                  op0=ALU.mult, op1=ALU.add)
                if k == "max1":
                    _, p, h, qb, half = item
                    w = min((qb + 1) * P, (half + 1) * QT) - half * QT
                    last = V.tensor_reduce(mx[:, h, qb, half:half + 1], m[:, 0:w], AX_X, ALU.max)
                if k == "max2":
                    _, g, h, qb, half = item
                    last = V.tensor_reduce(mx2[:, qb, half:half + 1], m[:, :], AX_X, ALU.max)
                if k == "dg1":
                    _, p, h, qt = item
                    if qt == 0:
                        dve.wait_ge(vec_done, c.after("vec_done", ("max1", p, h, NT - 1, 1)))
                        V.tensor_reduce(m8[:, h, :], mx[:, h], AX_X, ALU.max).then_inc(link, 1)
                        ch.wait()
                        V.tensor_scalar(m8n[:, h, :], m8[:, h, :], -1.0, None, ALU.mult).then_inc(link, 1)
                        ch.wait()
                        if c.known("s_ready", ("unit1", UP * p - UP + QT0_UNITS - 1)):
                            dve.wait_ge(s_ready, c.after("s_ready", ("unit1", UP * p - UP + QT0_UNITS - 1)))
                    else:
                        dve.wait_ge(s_ready, c.after("s_ready", ("unit1", UP * p - 1)))
                    last = V.tensor_tensor(
                        dg[:, 2 * h + qt, :].rearrange("p (t q) -> p t q", t=4),
                        ident[:].unsqueeze(1).to_broadcast([P, 4, P]),
                        m8n[:, h, 4 * qt:4 * qt + 4].unsqueeze(2).to_broadcast([P, 4, P]), ALU.mult)
                if k == "dg2":
                    _, g, h = item
                    dve.wait_ge(vec_done, c.after("vec_done", ("max2", g, h, NT - 1, 1)))
                    V.tensor_reduce(m8[:, 0, :], mx2[:], AX_X, ALU.max).then_inc(link, 1)
                    ch.wait()
                    V.tensor_scalar(m8n[:, 0, :], m8[:, 0, :], -1.0 / LOW_ONE, None, ALU.mult).then_inc(link, 1)
                    ch.wait()
                    u = ("unit1", UP * (PAIRS - 1) + QT0_UNITS - 1)
                    if c.known("s_ready", u):
                        dve.wait_ge(s_ready, c.after("s_ready", u))
                    for qt in range(2):
                        last = V.tensor_tensor(
                            dg[:, 2 * qt, :].rearrange("p (t q) -> p t q", t=4),
                            ident[:].unsqueeze(1).to_broadcast([P, 4, P]),
                            m8n[:, 0, 4 * qt:4 * qt + 4].unsqueeze(2).to_broadcast([P, 4, P]), ALU.mult)
                if k == "inj2":
                    _, g, h, qt = item
                    q = group_ops(g, h)[0][96:P, qt * QT:(qt + 1) * QT]
                    last = V.tensor_tensor(q, m[96:P, :], q.bitcast(F32), ALU.add)
                if k == "sum1":
                    _, p, qt = item
                    o = ot[:, p, qt * QT:(qt + 1) * QT]
                    V.reciprocal(o, m[:, :]).then_inc(link, 1)
                    ch.wait()
                    last = V.tensor_tensor(o, O[qt][:, :], o, ALU.mult)
                if k == "oproj":
                    half = item[1]
                    ts = slice(4 * half, 4 * half + 4)
                    tiles = range(4 * half, 4 * half + 4)
                    dve.wait_ge(out_stored, c.start("out_stored"))
                    dve.wait_ge(xb_loaded, c.after("xb_loaded", ("loadB",)))
                    layer_norm(ch, lambda t: m[:, (t % 4) * P:(t % 4 + 1) * P], lambda t: x1[:, t, :], tiles)\
                        .then_inc(link, 1)
                    ch.wait()
                    V.tensor_tensor(x1[:, ts, :], x1[:, ts, :], xb[:, ts, :], ALU.add).then_inc(link, 1)
                    ch.wait()
                    layer_norm(ch, lambda t: x1[:, t, :], lambda t: y1[:, t % 4, :], tiles).then_inc(link, 1)
                    ch.wait()
                    last = layer_norm(ch, lambda t: y1[:, t % 4, :], lambda t: xn[:, t, :], tiles)
                if k == "proj2":
                    t = item[1]
                    last = V.tensor_tensor(qkv2[:, t, :, :, 0:D2].rearrange("p w h d -> p (w h) d"),
                                           m[:, 0:3 * E].rearrange("p (w d) -> p w d", d=D2),
                                           bias2_bc[:].rearrange("p (w d) -> p w d", d=D2), ALU.add)
                if k == "o2T":
                    _, half, g = item
                    o = m[:, :].rearrange("p (t h d) -> p t h d", t=4, h=4)
                    V.reciprocal(rz[:], o[:, :, :, D2]).then_inc(link, 1)
                    ch.wait()
                    dst = xn[:, 4 * half:4 * half + 4, 64 * g:64 * g + 64].rearrange("p t (h d) -> p t h d", h=4)
                    last = V.tensor_tensor(dst, o[:, :, :, 0:D2], rz[:].unsqueeze(3).to_broadcast([P, 4, 4, D2]),
                                           ALU.mult)
                if k == "fproj":
                    half = item[1]
                    ts = slice(4 * half, 4 * half + 4)
                    tiles = range(4 * half, 4 * half + 4)
                    layer_norm(ch, lambda t: x1[:, t, :], lambda t: y1[:, t % 4, :], tiles).then_inc(link, 1)
                    ch.wait()
                    pairs = [(2 * e, width(4 * half + 2 * e)) for e in range(2)]
                    for t, w in pairs:
                        y = y1[:, t:t + 2, 0:w]
                        last = V.tensor_tensor(y, y, ob_bc[:, 0:w].unsqueeze(1).to_broadcast([P, 2, w]), ALU.add)
                    last.then_inc(link, 1)
                    ch.wait()
                    for t, w in pairs:
                        y = y1[:, t:t + 2, 0:w]
                        mt = m[:, t * P:(t + 2) * P].rearrange("p (t e) -> p t e", t=2)[:, :, 0:w]
                        last = V.tensor_tensor(y, y, mt, ALU.add)
                    last.then_inc(link, 1)
                    ch.wait()
                    layer_norm(ch, lambda t: y1[:, t % 4, :], lambda t: y1[:, t % 4, :], tiles)\
                        .then_inc(link, 1)
                    ch.wait()
                    last = V.tensor_tensor(x1[:, ts, :], x1[:, ts, :], y1[:], ALU.add)
                last.then_inc(vec_done, 1)

            def phase(c, b1, b2):
                for item in PHASES[c.phase]:
                    if "vec_done" in increments(item):
                        job(c, item)

            dve.wait_ge(w_loaded, 16 * WEIGHTS)
            dve.wait_ge(out_stored, 16)
            V.memset(mx[:], BIGNEG).then_inc(vec_consts, 1)
            V.tensor_copy(maskt[:], stage[:, 0, 0, :]).then_inc(vec_consts, 1)
            V.tensor_copy(identb[:], ident[:]).then_inc(vec_consts, 1)
            dve.wait_ge(vec_consts, 3)
            dve.wait_ge(const_done, 8)
            run(dve, phase)


def _constants(np):
    inv = (np.float32(1.0) / np.float32(10000.0) ** (np.arange(0, D1, 2, dtype=np.float32) / np.float32(D1)))
    ang = np.arange(T, dtype=np.float32)[:, None] * inv[None, :].astype(np.float32)
    cos, sin = np.cos(ang).astype(np.float32), np.sin(ang).astype(np.float32)
    split = np.zeros((P, 2), np.float32)
    split[64:, 0] = -1
    split[32:64, 1] = -1
    split[96:, 1] = -1
    return {
        "rope_c": cos, "rope_s": np.concatenate([-sin, sin], 1),
        "ident": np.eye(P, dtype=np.float32),
        "mask": np.tril(np.full((P, P), -1e30, np.float32), -1), "split": split,
    }


def kernel(**inputs):
    import numpy as np
    import concourse.bacc as _bacc
    from concourse.bass_utils import run_bass_kernel_spmd as _run

    a = {k: np.asarray(v) for k, v in inputs.items()}
    wq, wk = a["L0_attn_Wq"].T, a["L0_attn_Wk"].T
    hp = 2 * D1
    wqk = np.concatenate([w[:, p * hp:(p + 1) * hp] for p in range(PAIRS) for w in (wq, wk)], axis=1)
    k = _constants(np)
    arrays = {
        "x": a["L0_attn_x"].reshape(B * T, E), "wqk": wqk, "wv": a["L0_attn_Wv"].T, "wo": a["L0_attn_Wo"].T,
        "w2": np.concatenate([a[f"L0_ffn_{n}_w"].T for n in "qkv"], axis=1), "ow": a["L0_ffn_o_w"].T,
        "bias2": np.concatenate([a[f"L0_ffn_{n}_b"] for n in "qkv"]), "o_b": a["L0_ffn_o_b"],
        "norm_w": a["L0_ffn_norm_w"], "norm_b": a["L0_ffn_norm_b"],
        "rope_c": k["rope_c"], "rope_s": k["rope_s"], "ident_in": k["ident"], "mask_in": k["mask"],
        "split_in": k["split"],
    }
    arrays = {n: np.ascontiguousarray(v) for n, v in arrays.items()}
    nc = _bacc.Bacc("TRN2", target_bir_lowering=False, num_devices=1)
    args = [nc.dram_tensor(f"{n}_dram", v.shape, mybir.dt.from_np(v.dtype), kind="ExternalInput").ap()
            for n, v in arrays.items()]
    out = nc.dram_tensor("out_dram", (B * T, E), F32, kind="ExternalOutput").ap()
    causal_routed_kernel(nc, *args, out)
    r = _run(nc, [{f"{n}_dram": v for n, v in arrays.items()}], core_ids=[0])
    return r.results[0]["out_dram"].reshape(B, T, E)
```

```python
from contextlib import ExitStack

import concourse.bass as bass
from concourse import mybir

F32 = mybir.dt.float32
F32R = mybir.dt.float32r
BF16 = mybir.dt.bfloat16
ALU = mybir.AluOpType
ACT = mybir.ActivationFunctionType
AX_X = mybir.AxisListType.X

P = 128
B, T, E = 8, 1024, 128
H1, D1 = 8, 64
H2, D2 = 8, 16
EXPERTS = 4
NT = T // P
QT = 512
PAIRS, GROUPS = H1 // 2, H2 // 4
SCALE1, SCALE2 = D1 ** -0.5, E ** -0.5
EPS = 1e-5
NS, NP, NM = 3, 6, 3
NG = 3
UP, UG = 20, 64
SEL = 112
LOW_ONE = 2.0 ** -13
BIGNEG = -3.0e38


def width(t):
    return E >> (t * P // (T // EXPERTS))


def causal_units(qt):
    k = qt * 4
    return [[(kb, 0, 0)] for kb in range(k + 1)] + [[(k + 1, P, 0)], [(k + 2, 2 * P, 0), (k + 3, 3 * P, 2 * P)]]


UNITS1 = [(qt, blocks, h) for qt in range(2) for blocks in causal_units(qt) for h in range(2)]
assert len(UNITS1) == UP
QT0_UNITS = sum(qt == 0 for qt, _, _ in UNITS1)


def unit_width(blocks):
    kb, q0, c0 = blocks[-1]
    return c0 + QT - q0


def staged(jobs):
    out = [("stage", j) for j in jobs[:NG]]
    for n, j in enumerate(jobs):
        out += [j] + [("stage", k) for k in jobs[n + NG:n + NG + 1]]
    return out


def merged(a, b):
    out, k = [], 0
    for n, j in enumerate(a):
        out.append(j)
        while k * len(a) < len(b) * (n + 1):
            out.append(b[k])
            k += 1
    return out


def prep_pair(p):
    stacks = staged([("stk1", p, h, w, c) for h in range(2) for w in "qk" for c in range(2)])
    maxima = [[("max1", p, h, qb, c) for qb in range(NT) for c in range(2) if c == 0 or qb >= 4]
              + [("dg1", p, h, 0)] for h in range(2)]
    cut = stacks.index(("stk1", p, 0, "k", 1)) + 1
    return ([("qk", p, t2) for t2 in range(4)] + stacks[:cut] + merged(maxima[0], stacks[cut:]) + maxima[1])


def prep_group(g):
    stacks = staged([("stk2", g, h, w, c) for h in range(4) for w in "qk" for c in range(2)])
    cuts = [stacks.index(("stk2", g, h, "k", 1)) + 1 for h in range(4)]
    jobs = stacks[:cuts[0]]
    for h in range(4):
        maxima = [("max2", g, h, qb, c) for qb in range(NT) for c in range(2)]
        for n, k in enumerate({2: [0, 1], 3: [2]}.get(h, [])):
            maxima[9 * n:9 * n] = [("dg2", g, k)]
            maxima[9 * n + 4:9 * n + 4] = [("inj2", g, k, 0)]
            maxima[9 * n + 6:9 * n + 6] = [("inj2", g, k, 1)]
        jobs += merged(maxima, stacks[cuts[h]:cuts[h + 1]] if h < 3 else []) + [("neg2", g, h)]
    return jobs + [("dg2", g, 3), ("inj2", g, 3, 0), ("inj2", g, 3, 1)]


def norm_in_halves(n):
    return [(k, n, c) for k in ("stats", "norm") for c in range(2)]


TAKE_IN = norm_in_halves("x") + [("y0T", c) for c in range(2)]
VALUES = [("V", t) for t in range(NT)]
PROJECT = [("oproj", c) for c in range(2)] + norm_in_halves("proj")
MIDDLE = ([("x1", c) for c in range(2)] + norm_in_halves("y") + norm_in_halves("xn")
          + [("xnT", c) for c in range(2)] + [("proj2", t) for t in range(NT)])
TRANSPOSE_OUT = [("o2T", c, g) for c in range(2) for g in range(2)]
FINISH = ([("aoT", c) for c in range(2)] + [("resid", c) for c in range(2)] + [("fproj", c) for c in range(2)]
          + norm_in_halves("f") + [("add", c) for c in range(2)])
STORE = [("store", c) for c in range(2)]


COST = {"stage": 0.05, "qk": 2.0, "stk1": 0.6, "stk2": 0.6, "max1": 0.6, "max2": 0.6, "dg1": 0.9, "dg2": 1.3, "neg2": 0.4,
        "inj2": 0.8, "sum1": 0.9, "recip": 0.9, "scale": 0.7, "stats": 1.2, "norm": 0.8, "oproj": 3.6, "V": 0.9,
        "proj2": 0.7, "o2T": 0.8, "aoT": 0.5, "y0T": 0.5, "xnT": 0.5, "resid": 1.6, "fproj": 1.0, "add": 0.6,
        "x1": 0.6, "store": 0.0, "loadA": 0.0, "loadB": 0.0}


def beside(side, jobs, first, slots):
    total, spent = sum(COST[j[0]] for j in jobs), 0.0
    for j in jobs:
        side.setdefault(first + min(slots - 1, int(spent * slots / total)), []).append(j)
        spent += COST[j[0]]


def divide(p, qt):
    return [("sum1", p, qt)] + [("recip", p, qt, n) for n in range(4)] + [("scale", p, qt)]


def causal_phase(finish, middle):
    side = {}
    for p in range(PAIRS):
        for h in range(2):
            side.setdefault(UP * p + 1, []).append(("dg1", p, h, 1))
        if p:
            beside(side, divide(p - 1, 1), UP * p + 3, QT0_UNITS - 2)
    if finish:
        beside(side, TRANSPOSE_OUT + [("loadB",), ("loadA",)] + FINISH + STORE, 1, UP)
    else:
        side.setdefault(0, [])[:0] = [("loadB",), ("loadA",)] if middle else [("loadA",)]
    if middle:
        beside(side, MIDDLE, UP + 4, 2 * UP - 6)
    for p in range(PAIRS):
        beside(side, divide(p, 0), UP * p + QT0_UNITS + 3, UP - QT0_UNITS - 3)
        beside(side, prep_pair(p + 1) if p + 1 < PAIRS else prep_group(0) if middle else [], UP * p, UP)
    items = []
    assert all(j[0] != "dg2" for u in range(UP * (PAIRS - 1) + QT0_UNITS - 1) for j in side.get(u, []))
    for u in range(UP * PAIRS):
        items.append(("unit1", u))
        if u % 2 and u >= 3:
            items.append(("pv1", u - 3))
        items += side.get(u, [])
    return items + [("pv1", UP * PAIRS - 2)]


def routed_phase(causal_before):
    side = {}
    if causal_before:
        beside(side, divide(PAIRS - 1, 1), 0, 5)
        beside(side, TAKE_IN, 5, UG // 2)
    beside(side, prep_group(1), 0, UG)
    if causal_before:
        beside(side, VALUES + PROJECT, UG, UG - 4)
        beside(side, prep_pair(0), UG, UG)
    side.setdefault(UG - 2, []).append(("oev", 0, 0))
    side.setdefault(UG + 2, []).append(("oev", 0, 1))
    side.setdefault(2 * UG - 2, []).append(("oev", 1, 0))
    items = []
    for u in range(UG * GROUPS):
        items.append(("unit2", u))
        if u % 4 == 1 and u >= 5:
            items.append(("pv2", u - 5))
        items += side.get(u, [])
    return items + [("pv2", UG * GROUPS - 4), ("oev", 1, 1)]


PHASES = {
    "first": [("x1_free",), ("loadA",)] + TAKE_IN + VALUES + prep_pair(0),
    "causal0": causal_phase(False, False),
    "second": divide(PAIRS - 1, 1) + PROJECT + TAKE_IN + VALUES + prep_pair(0),
    "causal1": causal_phase(False, True),
    "routed0": routed_phase(True),
    "causal": causal_phase(True, True),
    "routed": routed_phase(True),
    "last": TRANSPOSE_OUT + [("loadB",)] + FINISH + STORE + MIDDLE + prep_group(0),
    "routed_last": routed_phase(False) + TRANSPOSE_OUT + FINISH + STORE,
}

LINKS = {"stats": 3, "dg1": 2, "neg2": 1, "o2T": 1, "resid": 1}
ACT_FREES = ("y0T", "V", "xnT", "aoT", "oproj", "stk1", "stk2", "sum1")
PE_JOBS = ("qk", "max1", "max2", "inj2", "proj2", "o2T", "fproj") + ACT_FREES


def key1(item):
    return item[0] == "stk1" and item[3] == "k"


def act_frees(item):
    return item[0] in ACT_FREES and not key1(item)


def increments(item):
    k = item[0]
    if k == "unit1":
        qt, blocks, _ = UNITS1[item[1] % UP]
        adds = {0: 0, 1: 2 - qt}.get(blocks[0][0], len(blocks))
        return {"s_ready": 1, "exp_done": 1, **({"sum_done": adds} if adds else {})}
    if k == "unit2":
        return {"s_ready": 1, "exp_done": 1}
    if k in ("pv1", "pv2"):
        return {"pv_done": 2 if k == "pv1" else 4}
    if k in ("loadA", "loadB"):
        return {"xa_loaded" if k == "loadA" else "xb_loaded": 16}
    if k == "x1_free":
        return {"out_stored": 16}
    if k == "store":
        return {"out_stored": 16}
    if k == "oev":
        return {"evac_done": 1}
    if k == "stage":
        return {"stage_done": 1, **({} if key1(item[1]) else {"low_done": 1})}
    out = {}
    if k in PE_JOBS:
        out["m_ready"] = 1
    if k in ACT_FREES:
        out["evac_done"] = 1
    if not act_frees(item):
        out["vec_done"] = 1
    if k == "qk":
        out["rope_done"] = 1
    if k == "stats":
        out["pow_done"] = 1
    links = LINKS.get(k, 0) if k != "dg1" or item[3] == 0 else 0
    if links:
        out["link"] = links
    return out


SEMS = ("s_ready", "exp_done", "sum_done", "pv_done", "m_ready", "evac_done", "vec_done", "rope_done",
        "link", "xa_loaded", "xb_loaded", "out_stored", "stage_done", "pow_done", "low_done")
TOTAL = {n: {s: sum(increments(i).get(s, 0) for i in items) for s in SEMS} for n, items in PHASES.items()}
AFTER = {}
for _n, _items in PHASES.items():
    _c = dict.fromkeys(SEMS, 0)
    for _i in _items:
        for _s, _k in increments(_i).items():
            _c[_s] += _k
            AFTER[_n, _s, _i] = _c[_s]


class Count:

    def __init__(self, phase, before, loop=None):
        self.phase, self.before, self.loop = phase, before, loop

    def plus(self, sem, k):
        v = sum(TOTAL[n][sem] for n in self.before) + k
        if self.loop is not None:
            v = self.loop * (TOTAL["causal"][sem] + TOTAL["routed"][sem]) + v
        return v

    def start(self, sem):
        return self.plus(sem, 0)

    def after(self, sem, item):
        return self.plus(sem, AFTER.get((self.phase, sem, item), 0))

    def known(self, sem, item):
        return (self.phase, sem, item) in AFTER


MISC = {n: [i for i in items if i[0] in PE_JOBS] for n, items in PHASES.items()}
MISC_AT = {n: {i: k for k, i in enumerate(items)} for n, items in MISC.items()}
STACKS = {n: [i for i in items if i[0] in ("stk1", "stk2")] for n, items in PHASES.items()}
ROPES = {n: [i for i in items if i[0] == "qk"] for n, items in PHASES.items()}


def causal_routed_kernel(nc, x, wqk, wv, wo, w2, ow, bias2, o_b, norm_w, norm_b, rope_c, rope_s,
                         ident_in, mask_in, out):
    with ExitStack() as ctx:
        def sb(name, shape, dt=F32):
            return ctx.enter_context(nc.sbuf_tensor(name, shape, dt))

        def bank(name):
            return ctx.enter_context(nc.psum_tensor(name, [P, QT], F32))

        wqk_sb = sb("wqk_sb", [P, PAIRS, 4 * D1])
        wv_sb = sb("wv_sb", [P, H1 * D1])
        wo_sb = sb("wo_sb", [P, PAIRS, E])
        w2_sb = sb("w2_sb", [P, 3 * E])
        ow_sb = sb("ow_sb", [P, E])
        bias2_bc = sb("bias2_bc", [P, 3 * E])
        ob_bc = sb("ob_bc", [P, E])
        norm_wb = sb("norm_wb", [P, 2])
        cos_sb = sb("cos_sb", [P, NT, D1 // 2])
        sin_sb = sb("sin_sb", [P, NT, D1])
        ident = sb("ident", [P, P])
        identb = sb("identb", [P, P], BF16)
        maskt = sb("maskt", [P, P], BF16)
        ones_r = sb("ones_r", [P, P], F32R)
        ones = ones_r[:, 0:D1].bitcast(F32)
        sel_r = sb("sel_r", [P, P], F32R)
        xa = sb("xa", [P, NT, E])
        xb = sb("xb", [P, NT, E])
        o2 = [xa, xb]
        x1 = sb("x1", [P, NT, E])
        xn = sb("xn", [P, NT, E])
        y0t = sb("y0t", [P, T])
        xnt = sb("xnt", [P, T])
        v1 = sb("v1", [P, NT, H1 * D1])
        rq = sb("rq", [P, NT, 4, D1])
        rtmp = sb("rtmp", [P, 2, 4, D1])
        stage = sb("stage", [P, NG, 4, P])
        stk = sb("stk", [P, 2, 8, T], F32R)
        qkv2 = sb("qkv2", [P, NT, 3, H2, 2 * D2])
        probs = sb("probs", [P, NP, QT])
        ot = sb("ot", [P, PAIRS, T])
        attn = ot[:, PAIRS - 1].rearrange("p (t e) -> p t e", t=NT)
        dg = sb("dg", [P, 4, QT], F32R)
        acc = sb("acc", [P, 2, 2, QT])
        mx = sb("mx", [P, 2, NT, 2])
        mx2 = sb("mx2", [P, 2, NT, 2])
        m8 = sb("m8", [P, 2, NT])
        m8n = sb("m8n", [P, 2, NT])
        m2n = sb("m2n", [P, 4, NT])
        st = sb("st", [P, NT, 6])
        sums = sb("sums", [P, NT, 2])
        diff = sb("diff", [P, NT])
        diff2 = sb("diff2", [P, NT])
        mean = sb("mean", [P, 2, NT])
        vpart = sb("vpart", [P, NT])
        zero = sb("zero", [P, 1])
        var = sb("var", [P, NT])
        rstd = sb("rstd", [P, 2, NT])
        neghalf = sb("neghalf", [P, NT])
        rz = sb("rz", [P, 4, 4])

        S = [bank(f"score{n}") for n in range(NS)]
        M = [bank(f"side{n}") for n in range(NM)]
        O = [bank(f"attn{n}") for n in range(2)]

        sems = {n: ctx.enter_context(nc.semaphore(n)) for n in SEMS}
        s_ready, exp_done, sum_done, pv_done = (sems[n] for n in SEMS[:4])
        m_ready, evac_done, vec_done, rope_done = (sems[n] for n in SEMS[4:8])
        link, xa_loaded, xb_loaded, out_stored, stage_done, pow_done, low_done = (sems[n] for n in SEMS[8:])
        w_loaded = ctx.enter_context(nc.semaphore("w_loaded"))
        const_done = ctx.enter_context(nc.semaphore("const_done"))
        vec_consts = ctx.enter_context(nc.semaphore("vec_consts"))

        def pair_ops(p, h):
            s = stk[:, p % 2]
            return s[:, 3 * h], s[:, 3 * h + 1], s[:, 3 * h + 2]

        def group_ops(g, h):
            s = stk[:, g % 2]
            return s[:, h], s[:, 4 + h]

        def misc(c, item):
            return M[MISC_AT[c.phase][item] % NM]

        WEIGHTS = 12

        def run(eng, phase):
            done = []
            for name, b1, b2 in (("first", 0, None), ("causal0", 0, None), ("second", 1, None),
                                 ("causal1", 1, 0), ("routed0", 1, 0)):
                phase(Count(name, list(done)), b1, b2)
                done.append(name)
            with eng.Fori(2, B) as i:
                before = list(done)
                phase(Count("causal", before, i - 2), i, i - 1)
                phase(Count("routed", before + ["causal"], i - 2), i, i - 1)
            done += ["causal", "routed"] * (B - 2)
            for name in ("last", "routed_last"):
                phase(Count(name, list(done)), None, B - 1)
                done.append(name)
            return done

        block = ctx.enter_context(nc.Block())

        @block.sync
        def _(sp):
            sp.dma_start(ident[:], ident_in).then_inc(out_stored, 16)
            for dst, src in ((wv_sb, wv), (w2_sb, w2), (ow_sb, ow)):
                sp.dma_start(dst[:], src).then_inc(w_loaded, 16)
            sp.dma_start(stage[:, 0, 0, :], mask_in).then_inc(w_loaded, 16)
            sp.dma_start(wqk_sb[:], wqk.rearrange("e (p n) -> e p n", p=PAIRS)).then_inc(w_loaded, 16)
            sp.dma_start(wo_sb[:], wo.rearrange("(p r) n -> r p n", r=P)).then_inc(w_loaded, 16)
            sp.dma_start(cos_sb[:], rope_c.rearrange("(t p) d -> p t d", p=P)).then_inc(w_loaded, 16)
            sp.dma_start(sin_sb[:], rope_s.rearrange("(t p) d -> p t d", p=P)).then_inc(w_loaded, 16)
            for dst, src in ((bias2_bc, bias2), (ob_bc, o_b)):
                sp.dma_start(dst[:], src.partition_broadcast(P)).then_inc(w_loaded, 16)
            for n, src in enumerate((norm_w, norm_b)):
                sp.dma_start(norm_wb[:, n:n + 1], src.unsqueeze(1)).then_inc(w_loaded, 16)

            xv = x.rearrange("(b t p) e -> b p t e", b=B, p=P)
            ov = out.rearrange("(b t p) e -> b p t e", b=B, p=P)

            def phase(c, b1, b2):
                for item in PHASES[c.phase]:
                    if item[0] in ("loadA", "loadB"):
                        sp.wait_ge(m_ready, c.after("m_ready", TRANSPOSE_OUT[-1]))
                    if item[0] == "loadA":
                        b = 0 if c.phase == "first" else (b1 + 1) % B
                        sp.dma_start(xa[:], xv[b]).then_inc(xa_loaded, 16)
                    if item[0] == "loadB":
                        sp.dma_start(xb[:], xv[b2]).then_inc(xb_loaded, 16)
                    if item[0] == "store":
                        half = item[1]
                        b = b2 if c.phase == "routed_last" else b2 - 1
                        sp.wait_ge(vec_done, c.after("vec_done", ("add", half)))
                        sp.dma_start(ov[b][:, 4 * half:4 * half + 4], x1[:, 4 * half:4 * half + 4, :])\
                            .then_inc(out_stored, 16)

            done = run(sp, phase)
            sp.wait_ge(out_stored, sum(TOTAL[n]["out_stored"] for n in done))

        @block.tensor
        def _(pe):
            mm = nc.tensor.matmul

            def transpose4(dst, src_of):
                for t in range(4):
                    last = nc.tensor.transpose(dst[:, t * P:(t + 1) * P], src_of(t), ident[:])
                return last

            def unit1(c, item):
                u = item[1]
                p, (qt, blocks, h) = u // UP, UNITS1[u % UP]
                q_op, k_hi, k_lo = pair_ops(p, h)
                if u >= NS:
                    pe.wait_ge(exp_done, c.after("exp_done", ("unit1", u - NS)))
                pe.wait_ge(vec_done, c.after("vec_done", ("dg1", p, h, qt)))
                s = S[u % NS]
                for kb, q0, c0 in blocks:
                    n = QT - q0
                    ks = slice(kb * P, (kb + 1) * P)
                    qs = slice(qt * QT + q0, (qt + 1) * QT)
                    diagonal = kb >= 4 * qt
                    mm(s[:, c0:c0 + n], k_hi[:, ks], q_op[:, qs], start=True, stop=False)
                    mm(s[:, c0:c0 + n], k_lo[:, ks], q_op[:, qs], start=False, stop=False)
                    last = mm(s[:, c0:c0 + n], ones_r[:], dg[:, 2 * h + qt, q0:], start=False, stop=True)
                    if diagonal:
                        last = mm(s[:, c0:c0 + P], identb[:], maskt[:], start=False, stop=True,
                                  skip_group_check=True)
                last.then_inc(s_ready, 1)

            def pv1(c, item):
                u0 = item[1]
                p, (qt, blocks, _) = u0 // UP, UNITS1[u0 % UP]
                pe.wait_ge(exp_done, c.after("exp_done", ("unit1", u0 + 1)))
                if blocks[0][0] == 0:
                    before = ("scale", p - 1, qt)
                    if c.known("vec_done", before):
                        pe.wait_ge(vec_done, c.after("vec_done", before))
                    else:
                        pe.wait_ge(evac_done, c.start("evac_done"))
                o = O[qt]
                for n, (kb, q0, c0) in enumerate(blocks):
                    for h in range(2):
                        last = mm(o[D1 * h:D1 * h + D1, q0:], v1[:, kb, (2 * p + h) * D1:(2 * p + h + 1) * D1],
                                  probs[:, (u0 + h) % NP, c0:c0 + QT - q0], start=(kb == 0),
                                  stop=(kb == 4 * qt + 3), skip_group_check=True)
                last.then_inc(pv_done, 2)

            def unit2(c, item):
                u = item[1]
                g, kb, qt, h = u // UG, u % UG // 8, u % 8 // 4, u % 4
                if u >= NS:
                    pe.wait_ge(exp_done, c.after("exp_done", ("unit2", u - NS)))
                if kb == 0:
                    pe.wait_ge(vec_done, c.after("vec_done", ("inj2", g, h, 1)))
                q_op, k_op = group_ops(g, h)
                mm(S[u % NS][:, :], k_op[:, kb * P:(kb + 1) * P], q_op[:, qt * QT:(qt + 1) * QT],
                   start=True, stop=True).then_inc(s_ready, 1)

            def pv2(c, item):
                u0 = item[1]
                g, kb, qt = u0 // UG, u0 % UG // 8, u0 % 8 // 4
                pe.wait_ge(exp_done, c.after("exp_done", ("unit2", u0 + 3)))
                if kb == 0 and not g and qt:
                    pe.wait_ge(vec_done, c.after("vec_done", ("scale", PAIRS - 1, 1)))
                if kb == 0 and g:
                    pe.wait_ge(evac_done, c.after("evac_done", ("oev", g - 1, qt)))
                for h in range(4):
                    last = mm(O[qt][32 * h:32 * h + 32, :], qkv2[:, kb, 2, 4 * g + h, :],
                              probs[:, (u0 + h) % NP, :], start=(kb == 0), stop=(kb == NT - 1),
                              skip_group_check=True)
                last.then_inc(pv_done, 4)

            def job(c, item):
                k = item[0]
                n = MISC_AT[c.phase][item]
                m = M[n % NM]
                if n >= NM:
                    old = MISC[c.phase][n - NM]
                    if act_frees(old):
                        pe.wait_ge(evac_done, c.after("evac_done", old))
                    else:
                        pe.wait_ge(vec_done, c.after("vec_done", old))
                if k == "y0T":
                    pe.wait_ge(vec_done, c.after("vec_done", ("norm", "x", item[1])))
                    last = transpose4(m, lambda t: xa[:, 4 * item[1] + t, :])
                if k == "V":
                    t = item[1]
                    pe.wait_ge(evac_done, c.after("evac_done", ("y0T", t // 4)))
                    last = mm(m[:, :], y0t[:, t * P:(t + 1) * P], wv_sb[:], start=True, stop=True)
                if k == "qk":
                    _, p, t2 = item
                    if c.known("evac_done", ("y0T", 1)):
                        pe.wait_ge(evac_done, c.after("evac_done", ("y0T", 1)))
                    for j in range(2):
                        t = 2 * t2 + j
                        last = mm(m[:, 256 * j:256 * j + 256], y0t[:, t * P:(t + 1) * P], wqk_sb[:, p, :],
                                  start=True, stop=True)
                if k in ("stk1", "stk2"):
                    done, name = (stage_done, "stage_done") if key1(item) else (low_done, "low_done")
                    pe.wait_ge(done, c.after(name, ("stage", item)))
                    last = transpose4(m, lambda t: stage[:, STACKS[c.phase].index(item) % NG, t, :])
                if k == "max1":
                    _, p, h, qb, half = item
                    q_op, k_hi, _ = pair_ops(p, h)
                    pe.wait_ge(vec_done, c.after("vec_done", ("stk1", p, h, "k", 1)))
                    end = min((qb + 1) * P, (half + 1) * QT)
                    w = end - half * QT
                    diagonal = end == (qb + 1) * P
                    last = mm(m[:, 0:w], q_op[:, qb * P:(qb + 1) * P], k_hi[:, half * QT:end],
                              start=True, stop=True)
                    if diagonal:
                        last = mm(m[:, w - P:w], maskt[:], identb[:], start=False, stop=True,
                                  skip_group_check=True)
                if k == "sum1":
                    _, p, qt = item
                    u = UP * p + (QT0_UNITS if qt == 0 else UP) - 1
                    pe.wait_ge(sum_done, c.after("sum_done", ("unit1", u)))
                    for h in range(2):
                        last = mm(m[D1 * h:D1 * h + D1, :], ones, acc[:, qt, h, :], start=True, stop=True,
                                  skip_group_check=True)
                if k == "max2":
                    _, g, h, qb, half = item
                    q_op, k_op = group_ops(g, h)
                    pe.wait_ge(evac_done, c.after("evac_done", ("stk2", g, h, "k", 1)))
                    last = mm(m[:, :], q_op[:, qb * P:(qb + 1) * P], k_op[:, half * QT:(half + 1) * QT],
                              start=True, stop=True)
                if k == "inj2":
                    _, g, h, qt = item
                    pe.wait_ge(vec_done, c.after("vec_done", ("dg2", g, h)))
                    last = mm(m[:, :], sel_r[:], dg[:, 2 * qt, :], start=True, stop=True)
                if k == "oproj":
                    pe.wait_ge(vec_done, c.after("vec_done", ("scale", PAIRS - 1, 1)))
                    for t in range(4):
                        q0 = (4 * item[1] + t) * P
                        for p in range(PAIRS):
                            last = mm(m[:, t * P:(t + 1) * P], ot[:, p, q0:q0 + P], wo_sb[:, p, :],
                                      start=(p == 0), stop=(p == PAIRS - 1))
                if k == "xnT":
                    pe.wait_ge(vec_done, c.after("vec_done", ("norm", "xn", item[1])))
                    last = transpose4(m, lambda t: xn[:, 4 * item[1] + t, :])
                if k == "proj2":
                    t = item[1]
                    w = width(t)
                    pe.wait_ge(evac_done, c.after("evac_done", ("xnT", t // 4)))
                    last = mm(m[:, 0:3 * E], xnt[0:w, t * P:(t + 1) * P], w2_sb[0:w, :], start=True, stop=True)
                if k == "o2T":
                    _, half, g = item
                    pe.wait_ge(evac_done, c.after("evac_done", ("oev", g, half)))
                    last = transpose4(m, lambda t: o2[g][:, 4 * half + t, :])
                if k == "aoT":
                    pe.wait_ge(vec_done, c.after("vec_done", ("o2T", item[1], 1)))
                    last = transpose4(m, lambda t: xn[:, 4 * item[1] + t, :])
                if k == "fproj":
                    pe.wait_ge(evac_done, c.after("evac_done", ("aoT", item[1])))
                    for j in range(4):
                        t = 4 * item[1] + j
                        w = width(t)
                        last = mm(m[:, j * P:j * P + w], xnt[0:w, t * P:(t + 1) * P], ow_sb[0:w, 0:w],
                                  start=True, stop=True)
                last.then_inc(m_ready, 1)

            def phase(c, b1, b2):
                pe.wait_ge(exp_done, c.start("exp_done"))
                pe.wait_ge(vec_done, c.start("vec_done"))
                pe.wait_ge(evac_done, c.start("evac_done"))
                for item in PHASES[c.phase]:
                    if item[0] == "unit1":
                        unit1(c, item)
                    elif item[0] == "unit2":
                        unit2(c, item)
                    elif item[0] == "pv1":
                        pv1(c, item)
                    elif item[0] == "pv2":
                        pv2(c, item)
                    elif item[0] in PE_JOBS:
                        job(c, item)

            pe.wait_ge(w_loaded, 16 * WEIGHTS)
            pe.wait_ge(out_stored, 16)
            pe.wait_ge(vec_consts, 3)
            pe.wait_ge(const_done, 8)
            run(pe, phase)

        def wait_for_source(eng, c, item):
            _, b, h, w, half = item
            if item[0] == "stk1":
                eng.wait_ge(rope_done, c.after("rope_done", ("qk", b, 2 * half + 1)))
            else:
                eng.wait_ge(vec_done, c.after("vec_done", ("proj2", 4 * half + 3)))

        def staging(c, item):
            _, b, h, w, half = item
            ts = slice(4 * half, 4 * half + 4)
            tile = stage[:, STACKS[c.phase].index(item) % NG]
            if item[0] == "stk1":
                src, times, d = rq[:, ts, "qk".index(w) * 2 + h, :], 2 if w == "k" else 1, D1
                parts = tile.rearrange("p t (w r d) -> p t w r d", w=2, r=1)
            else:
                src, times, d = qkv2[:, ts, "qk".index(w), 4 * b + h, :], 2, 2 * D2
                parts = tile.rearrange("p t (w r d) -> p t w r d" if w == "q" else "p t (r w d) -> p t w r d",
                                       w=2, r=2)
            src = src.unsqueeze(2).to_broadcast([P, 4, times, d])
            return src, parts[:, :, 0].bitcast(F32R), parts[:, :, 1]

        @block.scalar
        def _(act):
            def unit(c, item):
                k, u = item
                w = QT if k == "unit2" else unit_width(UNITS1[u % UP][1])
                act.wait_ge(s_ready, c.after("s_ready", item))
                if u >= NP:
                    if k == "unit1":
                        act.wait_ge(pv_done, c.after("pv_done", ("pv1", (u - NP) // 2 * 2)))
                        first = UNITS1[(u - NP) % UP][1][0][0] == 0
                        act.wait_ge(sum_done, c.after("sum_done", ("unit1", u - NP + 2 * first)))
                    else:
                        act.wait_ge(pv_done, c.after("pv_done", ("pv2", (u - NP) // 4 * 4)))
                nc.scalar.activation(probs[:, u % NP, 0:w], S[u % NS][:, 0:w], ACT.Exp,
                                     scale=SCALE1 if k == "unit1" else SCALE2).then_inc(exp_done, 1)

            def copy_to_stage(c, item):
                n = STACKS[c.phase].index(item[1])
                if n >= NG:
                    act.wait_ge(m_ready, c.after("m_ready", STACKS[c.phase][n - NG]))
                else:
                    act.wait_ge(m_ready, c.start("m_ready"))
                wait_for_source(act, c, item[1])
                src, hi, _ = staging(c, item[1])
                if key1(item[1]):
                    hi = stage[:, n % NG].rearrange("p t (r d) -> p t r d", r=2)
                nc.scalar.copy(hi, src).then_inc(stage_done, 1)

            def job(c, item):
                k = item[0]
                if k == "oev":
                    _, g, qt = item
                    act.wait_ge(pv_done, c.after("pv_done", ("pv2", UG * g + UG - 8 + 4 * qt)))
                    if g == 0 and c.known("m_ready", ("y0T", 1)):
                        act.wait_ge(m_ready, c.after("m_ready", ("y0T", 1)))
                    if g == 1:
                        act.wait_ge(vec_done, c.start("vec_done"))
                    nc.scalar.copy(o2[g][:, 4 * qt:4 * qt + 4, :], O[qt][:, :]).then_inc(evac_done, 1)
                    return
                m = misc(c, item)
                act.wait_ge(m_ready, c.after("m_ready", item))
                if k == "y0T":
                    dst = y0t[:, item[1] * QT:(item[1] + 1) * QT]
                if k == "V":
                    dst = v1[:, item[1], :]
                if k == "sum1":
                    dst = ot[:, item[1], item[2] * QT:(item[2] + 1) * QT]
                if k == "oproj":
                    dst = ot[:, PAIRS - 1, item[1] * QT:(item[1] + 1) * QT]
                if k in ("xnT", "aoT"):
                    dst = xnt[:, item[1] * QT:(item[1] + 1) * QT]
                if k in ("stk1", "stk2"):
                    _, b, h, w, half = item
                    ops = pair_ops(b, h) if k == "stk1" else group_ops(b, h)
                    dst = ops["qk".index(w)][:, half * QT:(half + 1) * QT]
                if k == "xnT":
                    nc.scalar.activation(dst, m[:, :], ACT.Identity, scale=norm_wb[:, 0:1],
                                         bias=norm_wb[:, 1:2]).then_inc(evac_done, 1)
                else:
                    nc.scalar.copy(dst, m[:, :]).then_inc(evac_done, 1)

            def phase(c, b1, b2):
                act.wait_ge(vec_done, c.start("vec_done"))
                act.wait_ge(pv_done, c.start("pv_done"))
                act.wait_ge(sum_done, c.start("sum_done"))
                for item in PHASES[c.phase]:
                    if item[0] in ("unit1", "unit2"):
                        unit(c, item)
                    elif item[0] == "stage":
                        copy_to_stage(c, item)
                    elif "evac_done" in increments(item):
                        job(c, item)

            act.wait_ge(w_loaded, 16 * WEIGHTS)
            act.wait_ge(out_stored, 16)
            act.wait_ge(vec_consts, 3)
            act.wait_ge(const_done, 8)
            run(act, phase)

        @block.gpsimd
        def _(pool):
            def unit1(c, item):
                u = item[1]
                p, (qt, blocks, h) = u // UP, UNITS1[u % UP]
                if blocks[0][0] == 0:
                    return
                pool.wait_ge(exp_done, c.after("exp_done", item))
                if blocks[0][0] == 1 and c.known("m_ready", ("sum1", p - 1, qt)):
                    pool.wait_ge(m_ready, c.after("m_ready", ("sum1", p - 1, qt)))
                a = acc[:, qt, h, :]
                if blocks[0][0] == 1:
                    first, src = probs[:, (u - 2) % NP, :], probs[:, u % NP, :]
                    q0 = blocks[0][1]
                    if q0:
                        nc.gpsimd.tensor_tensor(a[:, 0:q0], first[:, 0:q0], zero[:].to_broadcast([P, q0]), ALU.add)\
                            .then_inc(sum_done, 1)
                    nc.gpsimd.tensor_tensor(a[:, q0:], first[:, q0:], src[:, 0:QT - q0], ALU.add).then_inc(sum_done, 1)
                    return
                for n, (kb, q0, c0) in enumerate(blocks):
                    if n:
                        pool.wait_ge(sum_done, c.plus("sum_done", AFTER[c.phase, "sum_done", item] - 1))
                    else:
                        pool.wait_ge(sum_done, c.after("sum_done", ("unit1", u - 2)))
                    nc.gpsimd.tensor_tensor(a[:, q0:], a[:, q0:], probs[:, u % NP, c0:c0 + QT - q0], ALU.add)\
                        .then_inc(sum_done, 1)

            def qk(c, item):
                _, p, t2 = item
                pool.wait_ge(vec_done, c.after("vec_done", item))
                r = rq[:, 2 * t2:2 * t2 + 2].rearrange("p t h d -> p (t h d)")
                s = rtmp[:].rearrange("p t h d -> p (t h d)")
                nc.gpsimd.tensor_tensor(r, r, s, ALU.add).then_inc(rope_done, 1)

            def low_part(c, item):
                pool.wait_ge(stage_done, c.after("stage_done", item))
                wait_for_source(pool, c, item[1])
                src, hi, lo = staging(c, item[1])
                nc.gpsimd.tensor_tensor(lo, src, hi.bitcast(F32), ALU.subtract).then_inc(low_done, 1)

            def power(c, item):
                _, n, half = item
                tiles = slice(4 * half, 4 * half + 4)
                pool.wait_ge(vec_done, c.after("vec_done", item))
                nc.gpsimd.tensor_tensor(rstd[:, int(n != "y"), tiles], var[:, tiles], neghalf[:, tiles], ALU.pow)\
                    .then_inc(pow_done, 1)

            def phase(c, b1, b2):
                pool.wait_ge(m_ready, c.start("m_ready"))
                for item in PHASES[c.phase]:
                    if item[0] == "unit1":
                        unit1(c, item)
                    elif item[0] == "qk":
                        qk(c, item)
                    elif item[0] == "stats":
                        power(c, item)
                    elif item[0] == "stage" and not key1(item[1]):
                        low_part(c, item)

            nc.gpsimd.memset(ones_r[:].bitcast(F32), 1.0).then_inc(const_done, 1)
            nc.gpsimd.memset(sel_r[:].bitcast(F32), 0.0).then_inc(const_done, 1)
            nc.gpsimd.memset(qkv2[:], 0.0).then_inc(const_done, 1)
            nc.gpsimd.memset(neghalf[:], -0.5).then_inc(const_done, 1)
            nc.gpsimd.memset(zero[:], 0.0).then_inc(const_done, 1)
            pool.wait_ge(const_done, 5)
            nc.gpsimd.memset(sel_r[:, SEL:SEL + 1].bitcast(F32), 1.0).then_inc(const_done, 1)
            nc.gpsimd.memset(qkv2[:, :, 1, :, D2:D2 + 1], 1.0 + LOW_ONE).then_inc(const_done, 1)
            nc.gpsimd.memset(qkv2[:, :, 2, :, D2:D2 + 1], 1.0).then_inc(const_done, 1)
            run(pool, phase)

        @block.vector
        def _(dve):
            V = nc.vector

            class Chain:

                def __init__(self, c, item):
                    self.c, self.item, self.n = c, item, 0

                def wait(self):
                    self.n += 1
                    all_links = increments(self.item)["link"]
                    at = AFTER[self.c.phase, "link", self.item] - all_links + self.n
                    dve.wait_ge(link, self.c.plus("link", at))

            def tiles_of(n):
                buffers = {"x": (xa, xa), "proj": (attn, attn), "y": (x1, xn), "xn": (xn, xn), "f": (xn, xn)}
                src, dst = buffers[n]
                return lambda t: src[:, t, :], lambda t: dst[:, t, :]

            def stats(c, ch, n, half):
                a = 4 * half
                ts = slice(a, a + 4)
                for t in range(a, a + 4):
                    last = V.bn_stats(st[:, t, :], tiles_of(n)[0](t))
                last.then_inc(link, 1)
                ch.wait()
                V.tensor_tensor(sums[:, ts, :], st[:, ts, 1:3], st[:, ts, 4:6], ALU.add)
                V.tensor_tensor(diff[:, ts], st[:, ts, 1], st[:, ts, 4], ALU.subtract).then_inc(link, 1)
                ch.wait()
                V.tensor_scalar(mean[:, int(n != "y"), ts], sums[:, ts, 0], 0.5, None, ALU.mult)
                V.tensor_scalar(vpart[:, ts], sums[:, ts, 1], 1.0 / E, EPS, ALU.mult, ALU.add)
                V.tensor_tensor(diff2[:, ts], diff[:, ts], diff[:, ts], ALU.mult).then_inc(link, 1)
                ch.wait()
                return V.scalar_tensor_tensor(out=var[:, ts], in0=diff2[:, ts], scalar=0.25, in1=vpart[:, ts],
                                              op0=ALU.mult, op1=ALU.add)

            def normalise(n, half):
                src, dst = tiles_of(n)
                for t in range(4 * half, 4 * half + 4):
                    last = V.tensor_scalar(dst(t), src(t), mean[:, int(n != "y"), t:t + 1],
                                           rstd[:, int(n != "y"), t:t + 1], ALU.subtract, ALU.mult)
                return last

            def job(c, item):
                k = item[0]
                ch = Chain(c, item)
                m = None
                if k in PE_JOBS:
                    m = misc(c, item)
                    dve.wait_ge(m_ready, c.after("m_ready", item))
                if k not in ("max1", "max2"):
                    dve.wait_ge(vec_done, c.plus("vec_done", AFTER[c.phase, "vec_done", item] - 1))
                if k == "stats":
                    _, n, half = item
                    if n == "x":
                        dve.wait_ge(xa_loaded, c.start("xa_loaded") if c.phase != "first" else 16)
                    if n == "proj":
                        dve.wait_ge(evac_done, c.after("evac_done", ("oproj", half)))
                    last = stats(c, ch, n, half)
                if k == "norm":
                    _, n, half = item
                    dve.wait_ge(pow_done, c.after("pow_done", ("stats", n, half)))
                    last = normalise(n, half)
                if k == "qk":
                    _, p, t2 = item
                    n = ROPES[c.phase].index(item)
                    if n:
                        dve.wait_ge(rope_done, c.after("rope_done", ROPES[c.phase][n - 1]))
                    mv4 = m[:, :].rearrange("p (t h d) -> p t h d", t=2, h=4)
                    s = rtmp[:]
                    hd = D1 // 2
                    ts = slice(2 * t2, 2 * t2 + 2)
                    cosb = cos_sb[:, ts, :].unsqueeze(2).to_broadcast([P, 2, 8, hd])
                    V.tensor_tensor(rq[:, ts].rearrange("p t h (x d) -> p t (h x) d", x=2),
                                    m[:, :].rearrange("p (t h d) -> p t h d", t=2, h=8), cosb, ALU.mult)
                    for lo, hi in ((0, hd), (hd, 0)):
                        sinb = sin_sb[:, ts, lo:lo + hd].unsqueeze(2).to_broadcast([P, 2, 4, hd])
                        last = V.tensor_tensor(s[:, :, :, lo:lo + hd], mv4[:, :, :, hi:hi + hd], sinb, ALU.mult)
                if k == "stk1":
                    _, p, h, _, half = item
                    dve.wait_ge(evac_done, c.after("evac_done", item))
                    _, hi, lo = pair_ops(p, h)
                    cs = slice(half * QT, (half + 1) * QT)
                    last = V.tensor_tensor(lo[:, cs], m[:, :], hi[:, cs].bitcast(F32), ALU.subtract)
                if k == "max1":
                    _, p, h, qb, half = item
                    w = min((qb + 1) * P, (half + 1) * QT) - half * QT
                    last = V.tensor_reduce(mx[:, h, qb, half:half + 1], m[:, 0:w], AX_X, ALU.max)
                if k == "max2":
                    _, g, h, qb, half = item
                    last = V.tensor_reduce(mx2[:, h % 2, qb, half:half + 1], m[:, :], AX_X, ALU.max)
                if k == "dg1":
                    _, p, h, qt = item
                    if qt == 0:
                        dve.wait_ge(vec_done, c.after("vec_done", ("max1", p, h, NT - 1, 1)))
                        V.tensor_reduce(m8[:, h, :], mx[:, h], AX_X, ALU.max).then_inc(link, 1)
                        ch.wait()
                        V.tensor_scalar(m8n[:, h, :], m8[:, h, :], -1.0, None, ALU.mult).then_inc(link, 1)
                        ch.wait()
                        if c.known("s_ready", ("unit1", UP * p - UP + QT0_UNITS - 1)):
                            dve.wait_ge(s_ready, c.after("s_ready", ("unit1", UP * p - UP + QT0_UNITS - 1)))
                    else:
                        dve.wait_ge(s_ready, c.after("s_ready", ("unit1", UP * p - 1)))
                    last = V.tensor_tensor(
                        dg[:, 2 * h + qt, :].rearrange("p (t q) -> p t q", t=4),
                        ident[:].unsqueeze(1).to_broadcast([P, 4, P]),
                        m8n[:, h, 4 * qt:4 * qt + 4].unsqueeze(2).to_broadcast([P, 4, P]), ALU.mult)
                if k == "neg2":
                    _, g, h = item
                    dve.wait_ge(vec_done, c.after("vec_done", ("max2", g, h, NT - 1, 1)))
                    V.tensor_reduce(m8[:, 0, :], mx2[:, h % 2], AX_X, ALU.max).then_inc(link, 1)
                    ch.wait()
                    last = V.tensor_scalar(m2n[:, h, :], m8[:, 0, :], -1.0 / LOW_ONE, None, ALU.mult)
                if k == "dg2":
                    _, g, h = item
                    if h:
                        dve.wait_ge(m_ready, c.after("m_ready", ("inj2", g, h - 1, 1)))
                    u = ("unit1", UP * (PAIRS - 1) + QT0_UNITS - 1)
                    if c.known("s_ready", u):
                        dve.wait_ge(s_ready, c.after("s_ready", u))
                    for qt in range(2):
                        last = V.tensor_tensor(
                            dg[:, 2 * qt, :].rearrange("p (t q) -> p t q", t=4),
                            ident[:].unsqueeze(1).to_broadcast([P, 4, P]),
                            m2n[:, h, 4 * qt:4 * qt + 4].unsqueeze(2).to_broadcast([P, 4, P]), ALU.mult)
                if k == "inj2":
                    _, g, h, qt = item
                    q = group_ops(g, h)[0][96:P, qt * QT:(qt + 1) * QT]
                    last = V.tensor_tensor(q, m[96:P, :], q.bitcast(F32), ALU.add)
                if k == "recip":
                    _, p, qt, n = item
                    dve.wait_ge(evac_done, c.after("evac_done", ("sum1", p, qt)))
                    o = ot[:, p, qt * QT + n * P:qt * QT + (n + 1) * P]
                    last = V.reciprocal(o, o)
                if k == "scale":
                    _, p, qt = item
                    dve.wait_ge(pv_done, c.after("pv_done", ("pv1", UP * p + (QT0_UNITS if qt == 0 else UP) - 2)))
                    o = ot[:, p, qt * QT:(qt + 1) * QT]
                    last = V.tensor_tensor(o, O[qt][:, :], o, ALU.mult)
                if k == "x1":
                    half = item[1]
                    ts = slice(4 * half, 4 * half + 4)
                    dve.wait_ge(out_stored, c.after("out_stored", STORE[-1]))
                    dve.wait_ge(xb_loaded, c.after("xb_loaded", ("loadB",)))
                    last = V.tensor_tensor(x1[:, ts, :], attn[:, ts, :], xb[:, ts, :], ALU.add)
                if k == "proj2":
                    t = item[1]
                    last = V.tensor_tensor(qkv2[:, t, :, :, 0:D2].rearrange("p w h d -> p (w h) d"),
                                           m[:, 0:3 * E].rearrange("p (w d) -> p w d", d=D2),
                                           bias2_bc[:].rearrange("p (w d) -> p w d", d=D2), ALU.add)
                if k == "o2T":
                    _, half, g = item
                    o = m[:, :].rearrange("p (t h d) -> p t h d", t=4, h=4)
                    V.reciprocal(rz[:], o[:, :, :, D2]).then_inc(link, 1)
                    ch.wait()
                    dst = xn[:, 4 * half:4 * half + 4, 64 * g:64 * g + 64].rearrange("p t (h d) -> p t h d", h=4)
                    last = V.tensor_tensor(dst, o[:, :, :, 0:D2], rz[:].unsqueeze(3).to_broadcast([P, 4, 4, D2]),
                                           ALU.mult)
                if k in ("resid", "fproj"):
                    half = item[1]
                    pairs = [(t, width(t)) for t in (4 * half, 4 * half + 2)]
                if k == "resid":
                    dve.wait_ge(m_ready, c.after("m_ready", ("aoT", half)))
                    normalise("y", half).then_inc(link, 1)
                    ch.wait()
                    for t, w in pairs:
                        y = xn[:, t:t + 2, 0:w]
                        last = V.tensor_tensor(y, y, ob_bc[:, 0:w].unsqueeze(1).to_broadcast([P, 2, w]), ALU.add)
                if k == "fproj":
                    for t, w in pairs:
                        y = xn[:, t:t + 2, 0:w]
                        mt = m[:, t % 4 * P:(t % 4 + 2) * P].rearrange("p (t e) -> p t e", t=2)[:, :, 0:w]
                        last = V.tensor_tensor(y, y, mt, ALU.add)
                if k == "add":
                    half = item[1]
                    ts = slice(4 * half, 4 * half + 4)
                    last = V.tensor_tensor(x1[:, ts, :], x1[:, ts, :], xn[:, ts, :], ALU.add)
                last.then_inc(vec_done, 1)

            def phase(c, b1, b2):
                for item in PHASES[c.phase]:
                    if "vec_done" in increments(item):
                        job(c, item)

            dve.wait_ge(w_loaded, 16 * WEIGHTS)
            dve.wait_ge(out_stored, 16)
            V.memset(mx[:], BIGNEG).then_inc(vec_consts, 1)
            V.tensor_copy(maskt[:], stage[:, 0, 0, :]).then_inc(vec_consts, 1)
            V.tensor_copy(identb[:], ident[:]).then_inc(vec_consts, 1)
            dve.wait_ge(vec_consts, 3)
            dve.wait_ge(const_done, 8)
            run(dve, phase)


def _constants(np):
    inv = (np.float32(1.0) / np.float32(10000.0) ** (np.arange(0, D1, 2, dtype=np.float32) / np.float32(D1)))
    ang = np.arange(T, dtype=np.float32)[:, None] * inv[None, :].astype(np.float32)
    cos, sin = np.cos(ang).astype(np.float32), np.sin(ang).astype(np.float32)
    return {
        "rope_c": cos, "rope_s": np.concatenate([-sin, sin], 1),
        "ident": np.eye(P, dtype=np.float32),
        "mask": np.tril(np.full((P, P), -1e30, np.float32), -1),
    }


def kernel(**inputs):
    import numpy as np
    import concourse.bacc as _bacc
    from concourse.bass_utils import run_bass_kernel_spmd as _run

    a = {k: np.asarray(v) for k, v in inputs.items()}
    wq, wk = a["L0_attn_Wq"].T, a["L0_attn_Wk"].T
    hp = 2 * D1
    wqk = np.concatenate([w[:, p * hp:(p + 1) * hp] for p in range(PAIRS) for w in (wq, wk)], axis=1)
    k = _constants(np)
    arrays = {
        "x": a["L0_attn_x"].reshape(B * T, E), "wqk": wqk, "wv": a["L0_attn_Wv"].T, "wo": a["L0_attn_Wo"].T,
        "w2": np.concatenate([a[f"L0_ffn_{n}_w"].T for n in "qkv"], axis=1), "ow": a["L0_ffn_o_w"].T,
        "bias2": np.concatenate([a[f"L0_ffn_{n}_b"] for n in "qkv"]), "o_b": a["L0_ffn_o_b"],
        "norm_w": a["L0_ffn_norm_w"], "norm_b": a["L0_ffn_norm_b"],
        "rope_c": k["rope_c"], "rope_s": k["rope_s"], "ident_in": k["ident"], "mask_in": k["mask"],
    }
    arrays = {n: np.ascontiguousarray(v) for n, v in arrays.items()}
    nc = _bacc.Bacc("TRN2", target_bir_lowering=False, num_devices=1)
    args = [nc.dram_tensor(f"{n}_dram", v.shape, mybir.dt.from_np(v.dtype), kind="ExternalInput").ap()
            for n, v in arrays.items()]
    out = nc.dram_tensor("out_dram", (B * T, E), F32, kind="ExternalOutput").ap()
    causal_routed_kernel(nc, *args, out)
    r = _run(nc, [{f"{n}_dram": v for n, v in arrays.items()}], core_ids=[0])
    return r.results[0]["out_dram"].reshape(B, T, E)
```

```python
from contextlib import ExitStack

import concourse.bass as bass
from concourse import mybir

F32 = mybir.dt.float32
F32R = mybir.dt.float32r
BF16 = mybir.dt.bfloat16
ALU = mybir.AluOpType
ACT = mybir.ActivationFunctionType
AX_X = mybir.AxisListType.X

P = 128
B, T, E = 8, 1024, 128
H1, D1 = 8, 64
H2, D2 = 8, 16
EXPERTS = 4
NT = T // P
QT = 512
PAIRS, GROUPS = H1 // 2, H2 // 4
SCALE1, SCALE2 = D1 ** -0.5, E ** -0.5
EPS = 1e-5
NB, NP = 6, 6
NG = 3
UP, UG = 20, 64
SEL = 96
BIGNEG = -3.0e38


def width(t):
    return E >> (t * P // (T // EXPERTS))


def causal_units(qt):
    k = qt * 4
    return [[(kb, 0, 0)] for kb in range(k + 1)] + [[(k + 1, P, 0)], [(k + 2, 2 * P, 0), (k + 3, 3 * P, 2 * P)]]


UNITS1 = [(qt, blocks, h) for qt in range(2) for blocks in causal_units(qt) for h in range(2)]
assert len(UNITS1) == UP
QT0_UNITS = sum(qt == 0 for qt, _, _ in UNITS1)


def unit_width(blocks):
    kb, q0, c0 = blocks[-1]
    return c0 + QT - q0


def staged(jobs, ahead):
    out = [("stage", j) for j in jobs[:ahead]]
    for n, j in enumerate(jobs):
        out += [j] + [("stage", k) for k in jobs[n + ahead:n + ahead + 1]]
    return out


def merged(a, b):
    out, k = [], 0
    for n, j in enumerate(a):
        out.append(j)
        while k * len(a) < len(b) * (n + 1):
            out.append(b[k])
            k += 1
    return out


def prep_pair(p):
    stacks = staged([("stk1", p, h, w, c) for h in range(2) for w in "qk" for c in range(2)], NG)
    maxima = [[("max1", p, h, qb, c) for qb in range(NT) for c in range(2) if c == 0 or qb >= 4]
              + [("dg1", p, h, 0)] for h in range(2)]
    cut = stacks.index(("stk1", p, 0, "k", 1)) + 1
    return stacks[:cut] + merged(maxima[0], stacks[cut:]) + merged(maxima[1], rotate(p + 1))


def rotate(p):
    return [("qk", p, t2) for t2 in range(4)] if p < PAIRS else []


def prep_group(g):
    stacks = staged([("stk2", g, h, w, c) for h in range(4) for w in "qk" for c in range(2)], 4)
    cuts = [stacks.index(("stk2", g, h, "k", 1)) + 1 for h in range(4)]
    jobs = stacks[:cuts[0]]
    for h in range(4):
        maxima = [("max2", g, h, qb, c) for qb in range(NT) for c in range(2)]
        for n, k in enumerate({2: [0, 1], 3: [2]}.get(h, [])):
            maxima[9 * n:9 * n] = [("dg2", g, k)]
            maxima[9 * n + 5:9 * n + 5] = [("inj2", g, k, 0)]
            maxima[9 * n + 6:9 * n + 6] = [("inj2", g, k, 1)]
        jobs += merged(maxima, stacks[cuts[h]:cuts[h + 1]] if h < 3 else []) + [("neg2", g, h)]
    return jobs + [("dg2", g, 3), ("inj2", g, 3, 0), ("inj2", g, 3, 1)]


def norm_in_halves(n):
    return [(k, n, c) for k in ("stats", "norm") for c in range(2)]


TAKE_IN = norm_in_halves("x") + [("y0T", c) for c in range(2)]
VALUES = [("V", t) for t in range(NT)]
PROJECT = [("oproj", c) for c in range(2)] + norm_in_halves("proj")
MIDDLE = ([("x1", c) for c in range(2)] + norm_in_halves("y") + norm_in_halves("xn")
          + [("xnT", c) for c in range(2)] + [("proj2", t) for t in range(NT)])
TRANSPOSE_OUT = [("o2T", c, g) for c in range(2) for g in range(2)]
FINISH = ([("aoT", c) for c in range(2)] + [("resid", c) for c in range(2)] + [("fproj", c) for c in range(2)]
          + norm_in_halves("f") + [("add", c) for c in range(2)])
STORE = [("store", c) for c in range(2)]


WEIGHT = {"stage": 0.05, "qk": 2.0, "stk1": 2.04, "stk2": 0.8, "max1": 0.51, "max2": 0.51, "dg1": 0.76,
        "dg2": 1.3, "neg2": 0.29, "inj2": 0.8, "sum1": 0.63, "recip": 0.9, "scale": 0.7, "stats": 1.2,
        "norm": 0.8, "oproj": 3.6, "V": 0.9, "proj2": 0.84, "o2T": 1.12, "aoT": 0.24, "y0T": 1.2,
        "xnT": 0.42, "resid": 7.68, "fproj": 1.0, "add": 0.6, "x1": 0.6, "store": 0.0, "loadA": 0.0,
        "loadB": 0.0, "repeat": 0.7}


def beside(side, jobs, first, slots):
    total, spent = sum(WEIGHT[j[0]] for j in jobs), 0.0
    for j in jobs:
        side.setdefault(first + min(slots - 1, int(spent * slots / total)), []).append(j)
        spent += WEIGHT[j[0]]


def divide(p, qt):
    return [("sum1", p, qt)] + [("recip", p, qt, n) for n in range(2)] + [("repeat", p, qt), ("scale", p, qt)]


def causal_phase(finish, middle, pairs=range(PAIRS)):
    side = {}
    for p in range(PAIRS):
        for h in range(2):
            side.setdefault(UP * p + 1, []).append(("dg1", p, h, 1))
        if p:
            beside(side, divide(p - 1, 1), UP * p + 2, QT0_UNITS - 1)
    if finish:
        beside(side, TRANSPOSE_OUT + [("loadB",), ("loadA",)] + FINISH + STORE, 1, UP)
    else:
        side.setdefault(0, [])[:0] = [("loadB",), ("loadA",)] if middle else [("loadA",)]
    if not middle:
        beside(side, TAKE_IN, UP * (PAIRS - 2), UP // 2)
        beside(side, rotate(0), UP * (PAIRS - 1) - 7, 6)
    if middle and not finish:
        beside(side, PROJECT, 0, 6)
    if middle:
        beside(side, MIDDLE, UP + 4, 2 * UP - 6)
    for p in range(PAIRS):
        beside(side, divide(p, 0), UP * p + QT0_UNITS + 3, UP - QT0_UNITS - 3)
        if p + 1 < PAIRS:
            prep = prep_pair(p + 1)
        else:
            prep = prep_group(0) if middle else prep_pair(0)
        beside(side, prep, UP * p, UP)
    items = []
    last_pair = UP * (PAIRS - 1)
    assert all(j[0] != "dg2" and (j[0] != "dg1" or j[1] or j[3])
               for u in range(last_pair, last_pair + QT0_UNITS - 1) for j in side.get(u, []))
    first, end = UP * pairs[0], UP * (pairs[-1] + 1)
    for u in range(first, end):
        items.append(("unit1", u))
        if u % 2 and u >= first + 3:
            items.append(("pv1", u - 3))
        items += side.get(u, [])
    return items + [("pv1", end - 2)]


def routed_phase(causal_before):
    side = {}
    if causal_before:
        beside(side, divide(PAIRS - 1, 1), 0, 5)
        beside(side, TAKE_IN, 20, UG - 24)
    beside(side, prep_group(1), 0, UG)
    if causal_before:
        beside(side, rotate(0), UG - 8, 8)
        beside(side, PROJECT + VALUES, UG, UG - 4)
        beside(side, prep_pair(0), UG, UG)
    side.setdefault(UG - 2, []).append(("oev", 0, 0))
    side.setdefault(UG + 2, []).append(("oev", 0, 1))
    side.setdefault(2 * UG - 2, []).append(("oev", 1, 0))
    items = []
    for u in range(UG * GROUPS):
        items.append(("unit2", u))
        if u % 4 == 1 and u >= 5:
            items.append(("pv2", u - 5))
        items += side.get(u, [])
    return items + [("pv2", UG * GROUPS - 4), ("oev", 1, 1)]


PHASES = {
    "first": [("x1_free",), ("loadA",)] + TAKE_IN + rotate(0) + merged(prep_pair(0), VALUES),
    "causal0": causal_phase(False, False, range(PAIRS - 1)),
    "causal0_end": causal_phase(False, False, range(PAIRS - 1, PAIRS)),
    "second": merged(VALUES, divide(PAIRS - 1, 1)),
    "causal1": causal_phase(False, True),
    "routed0": routed_phase(True),
    "causal": causal_phase(True, True),
    "routed": routed_phase(True),
    "last": TRANSPOSE_OUT + [("loadB",)] + FINISH + STORE + MIDDLE + prep_group(0),
    "routed_last": routed_phase(False) + TRANSPOSE_OUT + FINISH + STORE,
}

LINKS = {"stats": 3, "dg1": 2, "neg2": 1, "o2T": 1, "resid": 1}
ACT_FREES = ("y0T", "V", "xnT", "aoT", "oproj", "stk1", "stk2", "sum1", "repeat", "inj2")
PE_JOBS = ("qk", "max1", "max2", "proj2", "o2T", "fproj") + ACT_FREES


def key1(item):
    return item[0] == "stk1" and item[3] == "k"


def act_frees(item):
    return item[0] in ACT_FREES and not key1(item)


def increments(item):
    k = item[0]
    if k == "unit1":
        qt, blocks, _ = UNITS1[item[1] % UP]
        adds = {0: 0, 1: 2 - qt}.get(blocks[0][0], len(blocks))
        return {"s_ready": 1, "exp_done": 1, **({"sum_done": adds} if adds else {})}
    if k == "unit2":
        return {"s_ready": 1, "exp_done": 1}
    if k in ("pv1", "pv2"):
        return {"pv_done": 2 if k == "pv1" else 4}
    if k in ("loadA", "loadB"):
        return {"xa_loaded" if k == "loadA" else "xb_loaded": 16}
    if k == "x1_free":
        return {"out_stored": 16}
    if k == "store":
        return {"out_stored": 16}
    if k == "oev":
        return {"evac_done": 1}
    if k == "stage":
        return {"stage_done": 1, **({} if key1(item[1]) else {"low_done": 1})}
    out = {}
    if k in PE_JOBS:
        out["m_ready"] = 1
    if k in ACT_FREES:
        out["evac_done"] = 1
    if not act_frees(item):
        out["vec_done"] = 1
    if k == "qk":
        out["rope_done"] = 1
    if k == "stats":
        out["pow_done"] = 1
    links = LINKS.get(k, 0) if k != "dg1" or item[3] == 0 else 0
    if links:
        out["link"] = links
    return out


SEMS = ("s_ready", "exp_done", "sum_done", "pv_done", "m_ready", "evac_done", "vec_done", "rope_done",
        "link", "xa_loaded", "xb_loaded", "out_stored", "stage_done", "pow_done", "low_done")
TOTAL = {n: {s: sum(increments(i).get(s, 0) for i in items) for s in SEMS} for n, items in PHASES.items()}
AFTER = {}
for _n, _items in PHASES.items():
    _c = dict.fromkeys(SEMS, 0)
    for _i in _items:
        for _s, _k in increments(_i).items():
            _c[_s] += _k
            AFTER[_n, _s, _i] = _c[_s]


class Count:

    def __init__(self, phase, before, loop=None):
        self.phase, self.before, self.loop = phase, before, loop

    def plus(self, sem, k):
        v = sum(TOTAL[n][sem] for n in self.before) + k
        if self.loop is not None:
            v = self.loop * (TOTAL["causal"][sem] + TOTAL["routed"][sem]) + v
        return v

    def start(self, sem):
        return self.plus(sem, 0)

    def after(self, sem, item):
        return self.plus(sem, AFTER.get((self.phase, sem, item), 0))

    def known(self, sem, item):
        return (self.phase, sem, item) in AFTER


BANKED = {n: [i for i in items if i[0] in PE_JOBS + ("unit1", "unit2")] for n, items in PHASES.items()}
BANK_AT = {n: {i: k for k, i in enumerate(items)} for n, items in BANKED.items()}
STACKS = {n: [i for i in items if i[0] in ("stk1", "stk2")] for n, items in PHASES.items()}
ROPES = {n: [i for i in items if i[0] == "qk"] for n, items in PHASES.items()}


def causal_routed_kernel(nc, x, wqk, wv, wo, w2, ow, bias2, o_b, norm_w, norm_b, rope_c, rope_s,
                         ident_in, mask_in, out):
    with ExitStack() as ctx:
        def sb(name, shape, dt=F32):
            return ctx.enter_context(nc.sbuf_tensor(name, shape, dt))

        def bank(name):
            return ctx.enter_context(nc.psum_tensor(name, [P, QT], F32))

        wqk_sb = sb("wqk_sb", [P, PAIRS, 4 * D1])
        wv_sb = sb("wv_sb", [P, H1 * D1])
        wo_sb = sb("wo_sb", [P, PAIRS, E])
        w2_sb = sb("w2_sb", [P, 3 * E])
        ow_sb = sb("ow_sb", [P, E])
        bias2_bc = sb("bias2_bc", [P, 3 * E])
        ob_bc = sb("ob_bc", [P, E])
        norm_wb = sb("norm_wb", [P, 2])
        cos_sb = sb("cos_sb", [P, NT, D1 // 2])
        sin_sb = sb("sin_sb", [P, NT, D1])
        ident = sb("ident", [P, P])
        identb = sb("identb", [P, P], BF16)
        maskt = sb("maskt", [P, P], BF16)
        ones_r = sb("ones_r", [P, P], F32R)
        sel_r = sb("sel_r", [P, P], F32R)
        xa = sb("xa", [P, NT, E])
        xb = sb("xb", [P, NT, E])
        o2 = [xa, xb]
        x1 = sb("x1", [P, NT, E])
        xn = sb("xn", [P, NT, E])
        y0t = sb("y0t", [P, T])
        xnt = sb("xnt", [P, T])
        v1 = sb("v1", [P, NT, H1 * D1])
        rq = sb("rq", [P, NT, 4, D1])
        rtmp = sb("rtmp", [P, 2, 4, D1])
        stage = sb("stage", [P, NG, 4, P])
        stk = sb("stk", [P, 2, 8, T], F32R)
        stage2 = sb("stage2", [P, 2, 2, 4, P])
        qk2 = sb("qk2", [P, NT, 2, H2, D2])
        v2 = sb("v2", [P, NT, H2, 2 * D2])
        probs = sb("probs", [P, NP, QT])
        ot = sb("ot", [P, PAIRS, T])
        attn = ot[:, PAIRS - 1].rearrange("p (t e) -> p t e", t=NT)
        dg = sb("dg", [P, 4, QT], F32R)
        acc = sb("acc", [P, 2, 2, QT])
        mx = sb("mx", [P, 2, NT, 2])
        mx2 = sb("mx2", [P, 2, NT, 2])
        m8 = sb("m8", [P, 2, NT])
        m8n = sb("m8n", [P, 2, NT])
        m2n = sb("m2n", [P, 4, NT])
        st = sb("st", [P, NT, 6])
        sums = sb("sums", [P, NT, 2])
        diff = sb("diff", [P, NT])
        diff2 = sb("diff2", [P, NT])
        mean = sb("mean", [P, 2, NT])
        vpart = sb("vpart", [P, NT])
        zero = sb("zero", [P, 1])
        var = sb("var", [P, NT])
        rstd = sb("rstd", [P, 2, NT])
        neghalf = sb("neghalf", [P, NT])
        rz = sb("rz", [P, 4, 4])

        ring = [bank(f"ring{n}") for n in range(NB)]
        O = [bank(f"attn{n}") for n in range(2)]

        sems = {n: ctx.enter_context(nc.semaphore(n)) for n in SEMS}
        s_ready, exp_done, sum_done, pv_done = (sems[n] for n in SEMS[:4])
        m_ready, evac_done, vec_done, rope_done = (sems[n] for n in SEMS[4:8])
        link, xa_loaded, xb_loaded, out_stored, stage_done, pow_done, low_done = (sems[n] for n in SEMS[8:])
        w_loaded = ctx.enter_context(nc.semaphore("w_loaded"))
        const_done = ctx.enter_context(nc.semaphore("const_done"))
        vec_consts = ctx.enter_context(nc.semaphore("vec_consts"))

        def pair_ops(p, h):
            s = stk[:, p % 2]
            return s[:, 3 * h], s[:, 3 * h + 1], s[:, 3 * h + 2]

        def group_ops(g, h):
            s = stk[:, g % 2]
            return s[:, h], s[:, 4 + h]

        def bank_of(c, item):
            return ring[BANK_AT[c.phase][item] % NB]

        def stage_tile(c, item):
            if item[0] == "stk2":
                return stage2[:, "qk".index(item[3]), item[4]]
            return stage[:, STACKS[c.phase].index(item) % NG]

        WEIGHTS = 12

        def run(eng, phase):
            done = []
            for name, b1, b2 in (("first", 0, None), ("causal0", 0, None), ("causal0_end", 0, None),
                                 ("second", 1, None),
                                 ("causal1", 1, 0), ("routed0", 1, 0)):
                phase(Count(name, list(done)), b1, b2)
                done.append(name)
            with eng.Fori(2, B) as i:
                before = list(done)
                phase(Count("causal", before, i - 2), i, i - 1)
                phase(Count("routed", before + ["causal"], i - 2), i, i - 1)
            done += ["causal", "routed"] * (B - 2)
            for name in ("last", "routed_last"):
                phase(Count(name, list(done)), None, B - 1)
                done.append(name)
            return done

        block = ctx.enter_context(nc.Block())

        @block.sync
        def _(sp):
            sp.dma_start(ident[:], ident_in).then_inc(out_stored, 16)
            for dst, src in ((wv_sb, wv), (w2_sb, w2), (ow_sb, ow)):
                sp.dma_start(dst[:], src).then_inc(w_loaded, 16)
            sp.dma_start(stage[:, 0, 0, :], mask_in).then_inc(w_loaded, 16)
            sp.dma_start(wqk_sb[:], wqk.rearrange("e (p n) -> e p n", p=PAIRS)).then_inc(w_loaded, 16)
            sp.dma_start(wo_sb[:], wo.rearrange("(p r) n -> r p n", r=P)).then_inc(w_loaded, 16)
            sp.dma_start(cos_sb[:], rope_c.rearrange("(t p) d -> p t d", p=P)).then_inc(w_loaded, 16)
            sp.dma_start(sin_sb[:], rope_s.rearrange("(t p) d -> p t d", p=P)).then_inc(w_loaded, 16)
            for dst, src in ((bias2_bc, bias2), (ob_bc, o_b)):
                sp.dma_start(dst[:], src.partition_broadcast(P)).then_inc(w_loaded, 16)
            for n, src in enumerate((norm_w, norm_b)):
                sp.dma_start(norm_wb[:, n:n + 1], src.unsqueeze(1)).then_inc(w_loaded, 16)

            xv = x.rearrange("(b t p) e -> b p t e", b=B, p=P)
            ov = out.rearrange("(b t p) e -> b p t e", b=B, p=P)

            def phase(c, b1, b2):
                for item in PHASES[c.phase]:
                    if item[0] in ("loadA", "loadB"):
                        sp.wait_ge(m_ready, c.after("m_ready", TRANSPOSE_OUT[-1]))
                    if item[0] == "loadA":
                        b = 0 if c.phase == "first" else (b1 + 1) % B
                        sp.dma_start(xa[:], xv[b]).then_inc(xa_loaded, 16)
                    if item[0] == "loadB":
                        sp.dma_start(xb[:], xv[b2]).then_inc(xb_loaded, 16)
                    if item[0] == "store":
                        half = item[1]
                        b = b2 if c.phase == "routed_last" else b2 - 1
                        sp.wait_ge(vec_done, c.after("vec_done", ("add", half)))
                        sp.dma_start(ov[b][:, 4 * half:4 * half + 4], x1[:, 4 * half:4 * half + 4, :])\
                            .then_inc(out_stored, 16)

            done = run(sp, phase)
            sp.wait_ge(out_stored, sum(TOTAL[n]["out_stored"] for n in done))

        @block.tensor
        def _(pe):
            mm = nc.tensor.matmul

            def transpose4(dst, src_of):
                for t in range(4):
                    last = nc.tensor.transpose(dst[:, t * P:(t + 1) * P], src_of(t), ident[:])
                return last

            def free_bank(c, item):
                n = BANK_AT[c.phase][item]
                if n >= NB:
                    old = BANKED[c.phase][n - NB]
                    if old[0] in ("unit1", "unit2"):
                        pe.wait_ge(exp_done, c.after("exp_done", old))
                    elif act_frees(old):
                        pe.wait_ge(evac_done, c.after("evac_done", old))
                    else:
                        pe.wait_ge(vec_done, c.after("vec_done", old))
                return ring[n % NB]

            def unit1(c, item):
                u = item[1]
                p, (qt, blocks, h) = u // UP, UNITS1[u % UP]
                s = free_bank(c, item)
                q_op, k_hi, k_lo = pair_ops(p, h)
                pe.wait_ge(vec_done, c.after("vec_done", ("dg1", p, h, qt)))
                for kb, q0, c0 in blocks:
                    n = QT - q0
                    ks = slice(kb * P, (kb + 1) * P)
                    qs = slice(qt * QT + q0, (qt + 1) * QT)
                    diagonal = kb >= 4 * qt
                    mm(s[:, c0:c0 + n], k_hi[:, ks], q_op[:, qs], start=True, stop=False)
                    mm(s[:, c0:c0 + n], k_lo[:, ks], q_op[:, qs], start=False, stop=False)
                    last = mm(s[:, c0:c0 + n], ones_r[:], dg[:, 2 * h + qt, q0:], start=False, stop=True)
                    if diagonal:
                        last = mm(s[:, c0:c0 + P], identb[:], maskt[:], start=False, stop=True,
                                  skip_group_check=True)
                last.then_inc(s_ready, 1)

            def pv1(c, item):
                u0 = item[1]
                p, (qt, blocks, _) = u0 // UP, UNITS1[u0 % UP]
                pe.wait_ge(exp_done, c.after("exp_done", ("unit1", u0 + 1)))
                if blocks[0][0] == 0:
                    before = ("scale", p - 1, qt)
                    if c.known("vec_done", before):
                        pe.wait_ge(vec_done, c.after("vec_done", before))
                    else:
                        pe.wait_ge(evac_done, c.start("evac_done"))
                o = O[qt]
                for n, (kb, q0, c0) in enumerate(blocks):
                    for h in range(2):
                        last = mm(o[D1 * h:D1 * h + D1, q0:], v1[:, kb, (2 * p + h) * D1:(2 * p + h + 1) * D1],
                                  probs[:, (u0 + h) % NP, c0:c0 + QT - q0], start=(kb == 0),
                                  stop=(kb == 4 * qt + 3), skip_group_check=True)
                last.then_inc(pv_done, 2)

            def unit2(c, item):
                u = item[1]
                g, kb, qt, h = u // UG, u % UG // 8, u % 8 // 4, u % 4
                s = free_bank(c, item)
                if kb == 0:
                    pe.wait_ge(evac_done, c.after("evac_done", ("inj2", g, h, 1)))
                q_op, k_op = group_ops(g, h)
                mm(s[:, :], k_op[:, kb * P:(kb + 1) * P], q_op[:, qt * QT:(qt + 1) * QT],
                   start=True, stop=True).then_inc(s_ready, 1)

            def pv2(c, item):
                u0 = item[1]
                g, kb, qt = u0 // UG, u0 % UG // 8, u0 % 8 // 4
                pe.wait_ge(exp_done, c.after("exp_done", ("unit2", u0 + 3)))
                if kb == 0 and not g and qt:
                    pe.wait_ge(vec_done, c.after("vec_done", ("scale", PAIRS - 1, 1)))
                if kb == 0 and g:
                    pe.wait_ge(evac_done, c.after("evac_done", ("oev", g - 1, qt)))
                for h in range(4):
                    last = mm(O[qt][32 * h:32 * h + 32, :], v2[:, kb, 4 * g + h, :],
                              probs[:, (u0 + h) % NP, :], start=(kb == 0), stop=(kb == NT - 1),
                              skip_group_check=True)
                last.then_inc(pv_done, 4)

            def job(c, item):
                k = item[0]
                m = free_bank(c, item)
                if k == "y0T":
                    pe.wait_ge(vec_done, c.after("vec_done", ("norm", "x", item[1])))
                    last = transpose4(m, lambda t: xa[:, 4 * item[1] + t, :])
                if k == "V":
                    t = item[1]
                    pe.wait_ge(evac_done, c.after("evac_done", ("y0T", t // 4)))
                    last = mm(m[:, :], y0t[:, t * P:(t + 1) * P], wv_sb[:], start=True, stop=True)
                if k == "qk":
                    _, p, t2 = item
                    if BANK_AT[c.phase].get(("y0T", 1), UG * 99) < BANK_AT[c.phase][item]:
                        pe.wait_ge(evac_done, c.after("evac_done", ("y0T", 1)))
                    for j in range(2):
                        t = 2 * t2 + j
                        last = mm(m[:, 256 * j:256 * j + 256], y0t[:, t * P:(t + 1) * P], wqk_sb[:, p, :],
                                  start=True, stop=True)
                if k in ("stk1", "stk2"):
                    done, name = (stage_done, "stage_done") if key1(item) else (low_done, "low_done")
                    pe.wait_ge(done, c.after(name, ("stage", item)))
                    last = transpose4(m, lambda t: stage_tile(c, item)[:, t, :])
                if k == "max1":
                    _, p, h, qb, half = item
                    q_op, k_hi, _ = pair_ops(p, h)
                    pe.wait_ge(evac_done, c.after("evac_done", ("stk1", p, h, "k", 1)))
                    end = min((qb + 1) * P, (half + 1) * QT)
                    w = end - half * QT
                    diagonal = end == (qb + 1) * P
                    last = mm(m[:, 0:w], q_op[:, qb * P:(qb + 1) * P], k_hi[:, half * QT:end],
                              start=True, stop=True)
                    if diagonal:
                        last = mm(m[:, w - P:w], maskt[:], identb[:], start=False, stop=True,
                                  skip_group_check=True)
                if k == "sum1":
                    _, p, qt = item
                    u = UP * p + (QT0_UNITS if qt == 0 else UP) - 1
                    pe.wait_ge(sum_done, c.after("sum_done", ("unit1", u)))
                    for n in range(4):
                        h, c0 = n // 2, n % 2 * QT // 2
                        last = mm(m[32 * n:32 * n + 32, 0:QT // 2], ones_r[:, 0:32].bitcast(F32),
                                  acc[:, qt, h, c0:c0 + QT // 2], start=True, stop=True, skip_group_check=True)
                if k == "repeat":
                    _, p, qt = item
                    pe.wait_ge(vec_done, c.after("vec_done", ("recip", p, qt, 1)))
                    for n in range(4):
                        h, c0 = n // 2, n % 2 * QT // 2
                        last = mm(m[D1 * h:D1 * h + D1, c0:c0 + QT // 2],
                                  ident[:, 32 * n:32 * n + 1].to_broadcast([P, D1]),
                                  ot[:, p, qt * QT:qt * QT + QT // 2], start=True, stop=True,
                                  skip_group_check=True)
                if k == "max2":
                    _, g, h, qb, half = item
                    q_op, k_op = group_ops(g, h)
                    pe.wait_ge(evac_done, c.after("evac_done", ("stk2", g, h, "k", 1)))
                    last = mm(m[:, :], q_op[:, qb * P:(qb + 1) * P], k_op[:, half * QT:(half + 1) * QT],
                              start=True, stop=True)
                if k == "inj2":
                    _, g, h, qt = item
                    pe.wait_ge(vec_done, c.after("vec_done", ("dg2", g, h)))
                    last = mm(m[:, :], sel_r[:], dg[:, 2 * qt, :], start=True, stop=True)
                if k == "oproj":
                    pe.wait_ge(vec_done, c.after("vec_done", ("scale", PAIRS - 1, 1)))
                    for t in range(4):
                        q0 = (4 * item[1] + t) * P
                        for p in range(PAIRS):
                            last = mm(m[:, t * P:(t + 1) * P], ot[:, p, q0:q0 + P], wo_sb[:, p, :],
                                      start=(p == 0), stop=(p == PAIRS - 1))
                if k == "xnT":
                    pe.wait_ge(vec_done, c.after("vec_done", ("norm", "xn", item[1])))
                    last = transpose4(m, lambda t: xn[:, 4 * item[1] + t, :])
                if k == "proj2":
                    t = item[1]
                    w = width(t)
                    pe.wait_ge(evac_done, c.after("evac_done", ("xnT", t // 4)))
                    last = mm(m[:, 0:3 * E], xnt[0:w, t * P:(t + 1) * P], w2_sb[0:w, :], start=True, stop=True)
                if k == "o2T":
                    _, half, g = item
                    pe.wait_ge(evac_done, c.after("evac_done", ("oev", g, half)))
                    last = transpose4(m, lambda t: o2[g][:, 4 * half + t, :])
                if k == "aoT":
                    pe.wait_ge(vec_done, c.after("vec_done", ("o2T", item[1], 1)))
                    last = transpose4(m, lambda t: xn[:, 4 * item[1] + t, :])
                if k == "fproj":
                    pe.wait_ge(evac_done, c.after("evac_done", ("aoT", item[1])))
                    for j in range(4):
                        t = 4 * item[1] + j
                        w = width(t)
                        last = mm(m[:, j * P:j * P + w], xnt[0:w, t * P:(t + 1) * P], ow_sb[0:w, 0:w],
                                  start=True, stop=True)
                last.then_inc(m_ready, 1)

            def phase(c, b1, b2):
                pe.wait_ge(exp_done, c.start("exp_done"))
                pe.wait_ge(vec_done, c.start("vec_done"))
                pe.wait_ge(evac_done, c.start("evac_done"))
                for item in PHASES[c.phase]:
                    if item[0] == "unit1":
                        unit1(c, item)
                    elif item[0] == "unit2":
                        unit2(c, item)
                    elif item[0] == "pv1":
                        pv1(c, item)
                    elif item[0] == "pv2":
                        pv2(c, item)
                    elif item[0] in PE_JOBS:
                        job(c, item)

            pe.wait_ge(w_loaded, 16 * WEIGHTS)
            pe.wait_ge(out_stored, 16)
            pe.wait_ge(vec_consts, 3)
            pe.wait_ge(const_done, 9)
            run(pe, phase)

        def wait_for_source(eng, c, item):
            _, b, h, w, half = item
            if item[0] == "stk1":
                eng.wait_ge(rope_done, c.after("rope_done", ("qk", b, 2 * half + 1)))
            else:
                eng.wait_ge(vec_done, c.after("vec_done", ("proj2", 4 * half + 3)))

        def staging(c, item):
            _, b, h, w, half = item
            ts = slice(4 * half, 4 * half + 4)
            tile = stage_tile(c, item)
            if item[0] == "stk1":
                src, times, d = rq[:, ts, "qk".index(w) * 2 + h, :], 2 if w == "k" else 1, D1
                parts = tile.rearrange("p t (w r d) -> p t w r d", w=2, r=1)
            else:
                src, times, d = qk2[:, ts, "qk".index(w), 4 * b + h, :], 2, D2
                parts = tile[:, :, 0:4 * D2].rearrange(
                    "p t (w r d) -> p t w r d" if w == "q" else "p t (r w d) -> p t w r d",
                    w=2, r=2)
            src = src.unsqueeze(2).to_broadcast([P, 4, times, d])
            return src, parts[:, :, 0].bitcast(F32R), parts[:, :, 1]

        @block.scalar
        def _(act):
            def unit(c, item):
                k, u = item
                w = QT if k == "unit2" else unit_width(UNITS1[u % UP][1])
                act.wait_ge(s_ready, c.after("s_ready", item))
                if u >= NP:
                    if k == "unit1":
                        act.wait_ge(pv_done, c.after("pv_done", ("pv1", (u - NP) // 2 * 2)))
                        first = UNITS1[(u - NP) % UP][1][0][0] == 0
                        act.wait_ge(sum_done, c.after("sum_done", ("unit1", u - NP + 2 * first)))
                    else:
                        act.wait_ge(pv_done, c.after("pv_done", ("pv2", (u - NP) // 4 * 4)))
                nc.scalar.activation(probs[:, u % NP, 0:w], bank_of(c, item)[:, 0:w], ACT.Exp,
                                     scale=SCALE1 if k == "unit1" else SCALE2).then_inc(exp_done, 1)

            def copy_to_stage(c, item):
                n = STACKS[c.phase].index(item[1])
                ahead = NG if item[1][0] == "stk1" else 4
                if n >= ahead:
                    act.wait_ge(m_ready, c.after("m_ready", STACKS[c.phase][n - ahead]))
                else:
                    act.wait_ge(m_ready, c.start("m_ready"))
                wait_for_source(act, c, item[1])
                src, hi, _ = staging(c, item[1])
                if key1(item[1]):
                    hi = stage_tile(c, item[1]).rearrange("p t (r d) -> p t r d", r=2)
                nc.scalar.copy(hi, src).then_inc(stage_done, 1)

            def job(c, item):
                k = item[0]
                if k == "oev":
                    _, g, qt = item
                    act.wait_ge(pv_done, c.after("pv_done", ("pv2", UG * g + UG - 8 + 4 * qt)))
                    if g == 0 and c.known("m_ready", ("y0T", 1)):
                        act.wait_ge(m_ready, c.after("m_ready", ("y0T", 1)))
                    if g == 1:
                        act.wait_ge(vec_done, c.start("vec_done"))
                    nc.scalar.copy(o2[g][:, 4 * qt:4 * qt + 4, :], O[qt][:, :]).then_inc(evac_done, 1)
                    return
                m = bank_of(c, item)
                act.wait_ge(m_ready, c.after("m_ready", item))
                if k == "y0T":
                    dst = y0t[:, item[1] * QT:(item[1] + 1) * QT]
                if k == "V":
                    dst = v1[:, item[1], :]
                if k == "sum1":
                    m = m[:, 0:QT // 2]
                    dst = ot[:, item[1], item[2] * QT:item[2] * QT + QT // 2]
                if k == "repeat":
                    dst = ot[:, item[1], item[2] * QT:(item[2] + 1) * QT]
                if k == "oproj":
                    dst = ot[:, PAIRS - 1, item[1] * QT:(item[1] + 1) * QT]
                if k in ("xnT", "aoT"):
                    dst = xnt[:, item[1] * QT:(item[1] + 1) * QT]
                if k == "inj2":
                    _, g, h, qt = item
                    m = m[SEL:P]
                    dst = group_ops(g, h)[0][SEL:P, qt * QT:(qt + 1) * QT]
                if k in ("stk1", "stk2"):
                    _, b, h, w, half = item
                    ops = pair_ops(b, h) if k == "stk1" else group_ops(b, h)
                    dst = ops["qk".index(w)][:, half * QT:(half + 1) * QT]
                if k == "xnT":
                    nc.scalar.activation(dst, m[:, :], ACT.Identity, scale=norm_wb[:, 0:1],
                                         bias=norm_wb[:, 1:2]).then_inc(evac_done, 1)
                else:
                    nc.scalar.copy(dst, m[:, :]).then_inc(evac_done, 1)

            def phase(c, b1, b2):
                act.wait_ge(vec_done, c.start("vec_done"))
                act.wait_ge(pv_done, c.start("pv_done"))
                act.wait_ge(sum_done, c.start("sum_done"))
                for item in PHASES[c.phase]:
                    if item[0] in ("unit1", "unit2"):
                        unit(c, item)
                    elif item[0] == "stage":
                        copy_to_stage(c, item)
                    elif "evac_done" in increments(item):
                        job(c, item)

            act.wait_ge(w_loaded, 16 * WEIGHTS)
            act.wait_ge(out_stored, 16)
            act.wait_ge(vec_consts, 3)
            act.wait_ge(const_done, 9)
            run(act, phase)

        @block.gpsimd
        def _(pool):
            def unit1(c, item):
                u = item[1]
                p, (qt, blocks, h) = u // UP, UNITS1[u % UP]
                if blocks[0][0] == 0:
                    return
                pool.wait_ge(exp_done, c.after("exp_done", item))
                if blocks[0][0] == 1 and c.known("m_ready", ("sum1", p - 1, qt)):
                    pool.wait_ge(m_ready, c.after("m_ready", ("sum1", p - 1, qt)))
                a = acc[:, qt, h, :]
                if blocks[0][0] == 1:
                    first, src = probs[:, (u - 2) % NP, :], probs[:, u % NP, :]
                    q0 = blocks[0][1]
                    if q0:
                        nc.gpsimd.tensor_tensor(a[:, 0:q0], first[:, 0:q0], zero[:].to_broadcast([P, q0]), ALU.add)\
                            .then_inc(sum_done, 1)
                    nc.gpsimd.tensor_tensor(a[:, q0:], first[:, q0:], src[:, 0:QT - q0], ALU.add).then_inc(sum_done, 1)
                    return
                for n, (kb, q0, c0) in enumerate(blocks):
                    if n:
                        pool.wait_ge(sum_done, c.plus("sum_done", AFTER[c.phase, "sum_done", item] - 1))
                    else:
                        pool.wait_ge(sum_done, c.after("sum_done", ("unit1", u - 2)))
                    nc.gpsimd.tensor_tensor(a[:, q0:], a[:, q0:], probs[:, u % NP, c0:c0 + QT - q0], ALU.add)\
                        .then_inc(sum_done, 1)

            def qk(c, item):
                _, p, t2 = item
                pool.wait_ge(vec_done, c.after("vec_done", item))
                r = rq[:, 2 * t2:2 * t2 + 2].rearrange("p t h d -> p (t h d)")
                s = rtmp[:].rearrange("p t h d -> p (t h d)")
                nc.gpsimd.tensor_tensor(r, r, s, ALU.add).then_inc(rope_done, 1)

            def low_part(c, item):
                pool.wait_ge(stage_done, c.after("stage_done", item))
                wait_for_source(pool, c, item[1])
                src, hi, lo = staging(c, item[1])
                nc.gpsimd.tensor_tensor(lo, src, hi.bitcast(F32), ALU.subtract).then_inc(low_done, 1)

            def power(c, item):
                _, n, half = item
                tiles = slice(4 * half, 4 * half + 4)
                pool.wait_ge(vec_done, c.after("vec_done", item))
                nc.gpsimd.tensor_tensor(rstd[:, int(n != "y"), tiles], var[:, tiles], neghalf[:, tiles], ALU.pow)\
                    .then_inc(pow_done, 1)

            def phase(c, b1, b2):
                pool.wait_ge(m_ready, c.start("m_ready"))
                for item in PHASES[c.phase]:
                    if item[0] == "unit1":
                        unit1(c, item)
                    elif item[0] == "qk":
                        qk(c, item)
                    elif item[0] == "stats":
                        power(c, item)
                    elif item[0] == "stage" and not key1(item[1]):
                        low_part(c, item)

            nc.gpsimd.memset(ones_r[:].bitcast(F32), 1.0).then_inc(const_done, 1)
            nc.gpsimd.memset(sel_r[:].bitcast(F32), 0.0).then_inc(const_done, 1)
            nc.gpsimd.memset(stage2[:], 0.0).then_inc(const_done, 1)
            nc.gpsimd.memset(v2[:], 0.0).then_inc(const_done, 1)
            nc.gpsimd.memset(neghalf[:], -0.5).then_inc(const_done, 1)
            nc.gpsimd.memset(zero[:], 0.0).then_inc(const_done, 1)
            pool.wait_ge(const_done, 6)
            nc.gpsimd.memset(sel_r[:, SEL:SEL + 1].bitcast(F32), 1.0).then_inc(const_done, 1)
            nc.gpsimd.memset(stage2[:, 1, :, :, SEL:SEL + 1], 1.0).then_inc(const_done, 1)
            nc.gpsimd.memset(v2[:, :, :, D2:D2 + 1], 1.0).then_inc(const_done, 1)
            run(pool, phase)

        @block.vector
        def _(dve):
            V = nc.vector

            class Chain:

                def __init__(self, c, item):
                    self.c, self.item, self.n = c, item, 0

                def wait(self):
                    self.n += 1
                    all_links = increments(self.item)["link"]
                    at = AFTER[self.c.phase, "link", self.item] - all_links + self.n
                    dve.wait_ge(link, self.c.plus("link", at))

            def tiles_of(n):
                buffers = {"x": (xa, xa), "proj": (attn, attn), "y": (x1, xn), "xn": (xn, xn), "f": (xn, xn)}
                src, dst = buffers[n]
                return lambda t: src[:, t, :], lambda t: dst[:, t, :]

            def stats(c, ch, n, half):
                a = 4 * half
                ts = slice(a, a + 4)
                for t in range(a, a + 4):
                    last = V.bn_stats(st[:, t, :], tiles_of(n)[0](t))
                last.then_inc(link, 1)
                ch.wait()
                V.tensor_tensor(sums[:, ts, :], st[:, ts, 1:3], st[:, ts, 4:6], ALU.add)
                V.tensor_tensor(diff[:, ts], st[:, ts, 1], st[:, ts, 4], ALU.subtract).then_inc(link, 1)
                ch.wait()
                V.tensor_scalar(mean[:, int(n != "y"), ts], sums[:, ts, 0], 0.5, None, ALU.mult)
                V.tensor_scalar(vpart[:, ts], sums[:, ts, 1], 1.0 / E, EPS, ALU.mult, ALU.add)
                V.tensor_tensor(diff2[:, ts], diff[:, ts], diff[:, ts], ALU.mult).then_inc(link, 1)
                ch.wait()
                return V.scalar_tensor_tensor(out=var[:, ts], in0=diff2[:, ts], scalar=0.25, in1=vpart[:, ts],
                                              op0=ALU.mult, op1=ALU.add)

            def normalise(n, half):
                src, dst = tiles_of(n)
                for t in range(4 * half, 4 * half + 4):
                    last = V.tensor_scalar(dst(t), src(t), mean[:, int(n != "y"), t:t + 1],
                                           rstd[:, int(n != "y"), t:t + 1], ALU.subtract, ALU.mult)
                return last

            def job(c, item):
                k = item[0]
                ch = Chain(c, item)
                m = None
                if k in PE_JOBS:
                    m = bank_of(c, item)
                    dve.wait_ge(m_ready, c.after("m_ready", item))
                if k not in ("max1", "max2"):
                    dve.wait_ge(vec_done, c.plus("vec_done", AFTER[c.phase, "vec_done", item] - 1))
                if k == "stats":
                    _, n, half = item
                    if n == "x":
                        dve.wait_ge(xa_loaded, c.after("xa_loaded", ("loadA",)))
                    if n == "proj":
                        dve.wait_ge(evac_done, c.after("evac_done", ("oproj", half)))
                    last = stats(c, ch, n, half)
                if k == "norm":
                    _, n, half = item
                    dve.wait_ge(pow_done, c.after("pow_done", ("stats", n, half)))
                    last = normalise(n, half)
                if k == "qk":
                    _, p, t2 = item
                    n = ROPES[c.phase].index(item)
                    if n:
                        dve.wait_ge(rope_done, c.after("rope_done", ROPES[c.phase][n - 1]))
                    mv4 = m[:, :].rearrange("p (t h d) -> p t h d", t=2, h=4)
                    s = rtmp[:]
                    hd = D1 // 2
                    ts = slice(2 * t2, 2 * t2 + 2)
                    cosb = cos_sb[:, ts, :].unsqueeze(2).to_broadcast([P, 2, 8, hd])
                    V.tensor_tensor(rq[:, ts].rearrange("p t h (x d) -> p t (h x) d", x=2),
                                    m[:, :].rearrange("p (t h d) -> p t h d", t=2, h=8), cosb, ALU.mult)
                    for lo, hi in ((0, hd), (hd, 0)):
                        sinb = sin_sb[:, ts, lo:lo + hd].unsqueeze(2).to_broadcast([P, 2, 4, hd])
                        last = V.tensor_tensor(s[:, :, :, lo:lo + hd], mv4[:, :, :, hi:hi + hd], sinb, ALU.mult)
                if k == "stk1":
                    _, p, h, _, half = item
                    dve.wait_ge(evac_done, c.after("evac_done", item))
                    _, hi, lo = pair_ops(p, h)
                    cs = slice(half * QT, (half + 1) * QT)
                    last = V.tensor_tensor(lo[:, cs], m[:, :], hi[:, cs].bitcast(F32), ALU.subtract)
                if k == "max1":
                    _, p, h, qb, half = item
                    w = min((qb + 1) * P, (half + 1) * QT) - half * QT
                    last = V.tensor_reduce(mx[:, h, qb, half:half + 1], m[:, 0:w], AX_X, ALU.max)
                if k == "max2":
                    _, g, h, qb, half = item
                    last = V.tensor_reduce(mx2[:, h % 2, qb, half:half + 1], m[:, :], AX_X, ALU.max)
                if k == "dg1":
                    _, p, h, qt = item
                    if qt == 0:
                        dve.wait_ge(vec_done, c.after("vec_done", ("max1", p, h, NT - 1, 1)))
                        V.tensor_reduce(m8[:, h, :], mx[:, h], AX_X, ALU.max).then_inc(link, 1)
                        ch.wait()
                        V.tensor_scalar(m8n[:, h, :], m8[:, h, :], -1.0, None, ALU.mult).then_inc(link, 1)
                        ch.wait()
                        u = UP * ((p - 1) % PAIRS) + QT0_UNITS - 1
                        if c.phase != "first":
                            dve.wait_ge(s_ready, c.after("s_ready", ("unit1", u)))
                    else:
                        dve.wait_ge(s_ready, c.after("s_ready", ("unit1", UP * p - 1)))
                    last = V.tensor_tensor(
                        dg[:, 2 * h + qt, :].rearrange("p (t q) -> p t q", t=4),
                        ident[:].unsqueeze(1).to_broadcast([P, 4, P]),
                        m8n[:, h, 4 * qt:4 * qt + 4].unsqueeze(2).to_broadcast([P, 4, P]), ALU.mult)
                if k == "neg2":
                    _, g, h = item
                    dve.wait_ge(vec_done, c.after("vec_done", ("max2", g, h, NT - 1, 1)))
                    V.tensor_reduce(m8[:, 0, :], mx2[:, h % 2], AX_X, ALU.max).then_inc(link, 1)
                    ch.wait()
                    last = V.tensor_scalar(m2n[:, h, :], m8[:, 0, :], -1.0, None, ALU.mult)
                if k == "dg2":
                    _, g, h = item
                    if h:
                        dve.wait_ge(m_ready, c.after("m_ready", ("inj2", g, h - 1, 1)))
                    u = ("unit1", UP * (PAIRS - 1) + QT0_UNITS - 1)
                    if c.known("s_ready", u):
                        dve.wait_ge(s_ready, c.after("s_ready", u))
                    for qt in range(2):
                        last = V.tensor_tensor(
                            dg[:, 2 * qt, :].rearrange("p (t q) -> p t q", t=4),
                            ident[:].unsqueeze(1).to_broadcast([P, 4, P]),
                            m2n[:, h, 4 * qt:4 * qt + 4].unsqueeze(2).to_broadcast([P, 4, P]), ALU.mult)
                if k == "recip":
                    _, p, qt, n = item
                    dve.wait_ge(evac_done, c.after("evac_done", ("sum1", p, qt)))
                    o = ot[:, p, qt * QT + n * P:qt * QT + (n + 1) * P]
                    last = V.reciprocal(o, o)
                if k == "scale":
                    _, p, qt = item
                    dve.wait_ge(evac_done, c.after("evac_done", ("repeat", p, qt)))
                    dve.wait_ge(pv_done, c.after("pv_done", ("pv1", UP * p + (QT0_UNITS if qt == 0 else UP) - 2)))
                    o = ot[:, p, qt * QT:(qt + 1) * QT]
                    last = V.tensor_tensor(o, O[qt][:, :], o, ALU.mult)
                if k == "x1":
                    half = item[1]
                    ts = slice(4 * half, 4 * half + 4)
                    dve.wait_ge(out_stored, c.after("out_stored", STORE[-1]))
                    dve.wait_ge(xb_loaded, c.after("xb_loaded", ("loadB",)))
                    last = V.tensor_tensor(x1[:, ts, :], attn[:, ts, :], xb[:, ts, :], ALU.add)
                if k == "proj2":
                    t = item[1]
                    V.tensor_tensor(qk2[:, t].rearrange("p w h d -> p (w h d)"), m[:, 0:2 * E],
                                    bias2_bc[:, 0:2 * E], ALU.add)
                    last = V.tensor_tensor(v2[:, t, :, 0:D2], m[:, 2 * E:3 * E].rearrange("p (h d) -> p h d", d=D2),
                                           bias2_bc[:, 2 * E:3 * E].rearrange("p (h d) -> p h d", d=D2), ALU.add)
                if k == "o2T":
                    _, half, g = item
                    o = m[:, :].rearrange("p (t h d) -> p t h d", t=4, h=4)
                    V.reciprocal(rz[:], o[:, :, :, D2]).then_inc(link, 1)
                    ch.wait()
                    dst = xn[:, 4 * half:4 * half + 4, 64 * g:64 * g + 64].rearrange("p t (h d) -> p t h d", h=4)
                    last = V.tensor_tensor(dst, o[:, :, :, 0:D2], rz[:].unsqueeze(3).to_broadcast([P, 4, 4, D2]),
                                           ALU.mult)
                if k in ("resid", "fproj"):
                    half = item[1]
                    pairs = [(t, width(t)) for t in (4 * half, 4 * half + 2)]
                if k == "resid":
                    dve.wait_ge(m_ready, c.after("m_ready", ("aoT", half)))
                    normalise("y", half).then_inc(link, 1)
                    ch.wait()
                    for t, w in pairs:
                        y = xn[:, t:t + 2, 0:w]
                        last = V.tensor_tensor(y, y, ob_bc[:, 0:w].unsqueeze(1).to_broadcast([P, 2, w]), ALU.add)
                if k == "fproj":
                    for t, w in pairs:
                        y = xn[:, t:t + 2, 0:w]
                        mt = m[:, t % 4 * P:(t % 4 + 2) * P].rearrange("p (t e) -> p t e", t=2)[:, :, 0:w]
                        last = V.tensor_tensor(y, y, mt, ALU.add)
                if k == "add":
                    half = item[1]
                    ts = slice(4 * half, 4 * half + 4)
                    last = V.tensor_tensor(x1[:, ts, :], x1[:, ts, :], xn[:, ts, :], ALU.add)
                last.then_inc(vec_done, 1)

            def phase(c, b1, b2):
                for item in PHASES[c.phase]:
                    if "vec_done" in increments(item):
                        job(c, item)

            dve.wait_ge(w_loaded, 16 * WEIGHTS)
            dve.wait_ge(out_stored, 16)
            V.memset(mx[:], BIGNEG).then_inc(vec_consts, 1)
            V.tensor_copy(maskt[:], stage[:, 0, 0, :]).then_inc(vec_consts, 1)
            V.tensor_copy(identb[:], ident[:]).then_inc(vec_consts, 1)
            dve.wait_ge(vec_consts, 3)
            dve.wait_ge(const_done, 9)
            run(dve, phase)


def _constants(np):
    inv = (np.float32(1.0) / np.float32(10000.0) ** (np.arange(0, D1, 2, dtype=np.float32) / np.float32(D1)))
    ang = np.arange(T, dtype=np.float32)[:, None] * inv[None, :].astype(np.float32)
    cos, sin = np.cos(ang).astype(np.float32), np.sin(ang).astype(np.float32)
    return {
        "rope_c": cos, "rope_s": np.concatenate([-sin, sin], 1),
        "ident": np.eye(P, dtype=np.float32),
        "mask": np.tril(np.full((P, P), -1e30, np.float32), -1),
    }


def kernel(**inputs):
    import numpy as np
    import concourse.bacc as _bacc
    from concourse.bass_utils import run_bass_kernel_spmd as _run

    a = {k: np.asarray(v) for k, v in inputs.items()}
    wq, wk = a["L0_attn_Wq"].T, a["L0_attn_Wk"].T
    hp = 2 * D1
    wqk = np.concatenate([w[:, p * hp:(p + 1) * hp] for p in range(PAIRS) for w in (wq, wk)], axis=1)
    k = _constants(np)
    arrays = {
        "x": a["L0_attn_x"].reshape(B * T, E), "wqk": wqk, "wv": a["L0_attn_Wv"].T, "wo": a["L0_attn_Wo"].T,
        "w2": np.concatenate([a[f"L0_ffn_{n}_w"].T for n in "qkv"], axis=1), "ow": a["L0_ffn_o_w"].T,
        "bias2": np.concatenate([a[f"L0_ffn_{n}_b"] for n in "qkv"]), "o_b": a["L0_ffn_o_b"],
        "norm_w": a["L0_ffn_norm_w"], "norm_b": a["L0_ffn_norm_b"],
        "rope_c": k["rope_c"], "rope_s": k["rope_s"], "ident_in": k["ident"], "mask_in": k["mask"],
    }
    arrays = {n: np.ascontiguousarray(v) for n, v in arrays.items()}
    nc = _bacc.Bacc("TRN2", target_bir_lowering=False, num_devices=1)
    args = [nc.dram_tensor(f"{n}_dram", v.shape, mybir.dt.from_np(v.dtype), kind="ExternalInput").ap()
            for n, v in arrays.items()]
    out = nc.dram_tensor("out_dram", (B * T, E), F32, kind="ExternalOutput").ap()
    causal_routed_kernel(nc, *args, out)
    r = _run(nc, [{f"{n}_dram": v for n, v in arrays.items()}], core_ids=[0])
    return r.results[0]["out_dram"].reshape(B, T, E)
```
